# Optimizing a Trainium2 kernel written in Bass

```python
import numpy as np
import jax
import jax.numpy as jnp

def _softmax(x, axis=-1):
    return jax.nn.softmax(x, axis=axis)

def _gelu(x):
    return jax.nn.gelu(x, approximate=True)

def _silu(x):
    return jax.nn.silu(x)

def _sigmoid(x):
    return jax.nn.sigmoid(x)

def _layernorm(x, axis=-1, eps=1e-05):
    m = jnp.mean(x, axis=axis, keepdims=True)
    v = jnp.var(x, axis=axis, keepdims=True)
    return (x - m) / jnp.sqrt(v + eps)

def _scatter_add(tgt, idx, src, axis=0):
    return tgt.at[idx].add(src)

def _segment_sum(src, seg, n):
    return jax.ops.segment_sum(src, seg, n)
kernel_name = 'mk_xattn_ffn_d2_seqx_r4_0936c1'

def setup_inputs(seed: int=0):
    np.random.seed(seed)
    _w = jnp.asarray

    def _rec_inputs():
        import jax
        import jax.numpy as jnp
        _rk = jax.random.key(seed)
        x = -0.0003929 + 0.9999 * jax.random.normal(jax.random.fold_in(_rk, 1), (4, 512, 512), jnp.float32)
        _lenS = 512 - jax.random.randint(jax.random.fold_in(_rk, 7), (4,), 0, max(1, 512 // 4) + 1, jnp.int32)
        _lenS2 = 1601 - jax.random.randint(jax.random.fold_in(_rk, 8), (4,), 0, max(1, 1601 // 4) + 1, jnp.int32)
        _ctx_2048P = jax.random.normal(jax.random.fold_in(_rk, 11), (4, 16, 512), jnp.float32)
        _ctx_2048c = jax.random.dirichlet(jax.random.fold_in(_rk, 511), 0.3 * jnp.ones((16,), jnp.float32), (4, 1601))
        _ctx_2048t = jnp.einsum('bsk,bkd->bsd', _ctx_2048c, _ctx_2048P)
        _ctx_2048t = _ctx_2048t * jax.lax.rsqrt(jnp.mean(jnp.square(_ctx_2048t)) + 1e-12) * 0.953939
        ctx_2048 = -0.000514642 + 1.00011 * (_ctx_2048t + 0.3 * jax.random.normal(jax.random.fold_in(_rk, 611), (4, 1601, 512), jnp.float32))
        _validS = jnp.arange(512)[None, :] < _lenS[:, None]
        _validS2 = jnp.arange(1601)[None, :] < _lenS2[:, None]
        _causal = jnp.tril(jnp.ones((512, 512), dtype=bool))
        mask_BxS2_ik0 = jnp.where(jnp.broadcast_to(_validS2[:, :], (4, 1601)), 0, 1).astype(jnp.int32)
        return (x, ctx_2048, mask_BxS2_ik0)
    x, ctx_2048, mask_BxS2_ik0 = _rec_inputs()

    def _L0_xattn_setup():
        import jax, jax.numpy as jnp
        import numpy as np
        NUM_HEADS = 16

        def _qdq(x):
            s = jnp.maximum(jnp.max(jnp.abs(x), axis=-1, keepdims=True) / 127.0, 1e-08)
            return jnp.clip(jnp.round(x / s), -127.0, 127.0) * s
        key = jax.random.key(seed)
        ks = jax.random.split(key, 8)
        B, N, M, D = (2, 1024, 128, 512)
        w_std = 0.02
        return {'x': jax.random.normal(ks[0], (B, N, D), jnp.float32), 'cond': jax.random.normal(ks[1], (B, M, D), jnp.float32), 'wq': jax.random.normal(ks[2], (D, D), jnp.float32) * w_std, 'bq': jax.random.normal(ks[3], (D,), jnp.float32) * w_std, 'wkv': jax.random.normal(ks[4], (2 * D, D), jnp.float32) * w_std, 'bkv': jax.random.normal(ks[5], (2 * D,), jnp.float32) * w_std, 'wp': jax.random.normal(ks[6], (D, D), jnp.float32) * w_std, 'bp': jax.random.normal(ks[7], (D,), jnp.float32) * w_std}
    _L0_xattn_all = _L0_xattn_setup()
    _L0_xattn_in = {k: v for k, v in _L0_xattn_all.items() if k in ('wq', 'bq', 'wkv', 'bkv', 'wp', 'bp')}
    del _L0_xattn_all

    def _L0_ffn_setup():
        import jax, jax.numpy as jnp
        import numpy as np
        D_MODEL = 512
        D_FF = 2048
        BATCH = 4
        SEQ = 512
        MAX_EXP = 4
        NUM_BITS = 8
        C_CHUNKS = 2
        SCALE = 0.1

        def _pow2_ternary(key, out_dim, in_dim, max_exp):
            k1, k2 = jax.random.split(key)
            t = jax.random.randint(k1, (out_dim, in_dim), -1, 2).astype(jnp.float32)
            e = jax.random.randint(k2, (out_dim, in_dim), 0, max_exp + 1).astype(jnp.float32)
            return t * jnp.exp2(-e)

        def _lookup_act(h):
            total_bits = NUM_BITS * C_CHUNKS
            qmax = 2 ** (total_bits - 1) - 1
            qmin = -2 ** (total_bits - 1)
            q = jnp.clip(jnp.round(h / SCALE), qmin, qmax)
            return jax.nn.gelu(q * SCALE)
        key = jax.random.key(seed)
        kx, k1, k2 = jax.random.split(key, 3)
        x = jax.random.normal(kx, (BATCH, SEQ, D_MODEL), dtype=jnp.float32)
        W1 = _pow2_ternary(k1, D_FF, D_MODEL, MAX_EXP)
        W2 = _pow2_ternary(k2, D_MODEL, D_FF, MAX_EXP)
        return {'x': x, 'W1': W1, 'W2': W2}
    _L0_ffn_all = _L0_ffn_setup()
    _L0_ffn_in = {k: v for k, v in _L0_ffn_all.items() if k in ('W1', 'W2')}
    del _L0_ffn_all

    def _L1_xattn_setup():
        import jax, jax.numpy as jnp
        import numpy as np
        import math
        H = 512
        NH = 16
        HD = H // NH
        EPS_LN = 1e-05
        RES_SCALE_MAX = 0.3

        def _nan_clean(x, lim=10000.0):
            return jnp.nan_to_num(x, nan=0.0, posinf=lim, neginf=-lim)
        key = jax.random.key(seed)
        ks = jax.random.split(key, 12)
        B, S, T = (4, 512, 64)
        std = 1.0 / math.sqrt(H)
        return {'hidden_states': jax.random.normal(ks[0], (B, S, H), jnp.float32), 'audio_tokens': jax.random.normal(ks[1], (B, T, H), jnp.float32), 'attention_mask': jax.random.randint(ks[2], (B, T), 0, 2, jnp.int32), 'Wq': jax.random.normal(ks[3], (H, H), jnp.float32) * std, 'bq': jnp.zeros((H,), jnp.float32), 'Wk': jax.random.normal(ks[4], (H, H), jnp.float32) * std, 'bk': jnp.zeros((H,), jnp.float32), 'Wv': jax.random.normal(ks[5], (H, H), jnp.float32) * std, 'bv': jnp.zeros((H,), jnp.float32), 'Wo': jax.random.normal(ks[6], (H, H), jnp.float32) * std, 'bo': jnp.zeros((H,), jnp.float32), 'ln_gamma': jnp.ones((H,), jnp.float32), 'ln_beta': jnp.zeros((H,), jnp.float32), 'residual_scale': jnp.float32(0.05)}
    _L1_xattn_all = _L1_xattn_setup()
    _L1_xattn_in = {k: v for k, v in _L1_xattn_all.items() if k in ('Wq', 'bq', 'Wk', 'bk', 'Wv', 'bv', 'Wo', 'bo', 'ln_gamma', 'ln_beta', 'residual_scale')}
    del _L1_xattn_all

    def _L1_ffn_setup():
        import jax, jax.numpy as jnp
        import numpy as np
        DIM = 512
        N_EXPERTS = 8
        TOP_K = 2
        key = jax.random.key(seed)
        ks = jax.random.split(key, 5)
        x = jax.random.normal(ks[0], (4, 1024, DIM), dtype=jnp.float32)
        W_up = jax.random.normal(ks[1], (DIM, DIM), dtype=jnp.float32) * (1.0 / np.sqrt(DIM))
        W_down = jax.random.normal(ks[2], (DIM, DIM), dtype=jnp.float32) * (1.0 / np.sqrt(DIM))
        W_gate = jax.random.normal(ks[3], (N_EXPERTS, DIM), dtype=jnp.float32) * (1.0 / np.sqrt(DIM))
        W_expert = jax.random.normal(ks[4], (DIM, DIM), dtype=jnp.float32) * (1.0 / np.sqrt(DIM))
        return {'x': x, 'W_up': W_up, 'W_down': W_down, 'W_gate': W_gate, 'W_expert': W_expert}
    _L1_ffn_all = _L1_ffn_setup()
    _L1_ffn_in = {k: v for k, v in _L1_ffn_all.items() if k in ('W_up', 'W_down', 'W_gate', 'W_expert')}
    del _L1_ffn_all
    return {'x': x, 'ctx_2048': ctx_2048, 'mask_BxS2_ik0': mask_BxS2_ik0, 'L0_xattn_wq': _L0_xattn_in['wq'], 'L0_xattn_bq': _L0_xattn_in['bq'], 'L0_xattn_wkv': _L0_xattn_in['wkv'], 'L0_xattn_bkv': _L0_xattn_in['bkv'], 'L0_xattn_wp': _L0_xattn_in['wp'], 'L0_xattn_bp': _L0_xattn_in['bp'], 'L0_ffn_W1': _L0_ffn_in['W1'], 'L0_ffn_W2': _L0_ffn_in['W2'], 'L1_xattn_Wq': _L1_xattn_in['Wq'], 'L1_xattn_bq': _L1_xattn_in['bq'], 'L1_xattn_Wk': _L1_xattn_in['Wk'], 'L1_xattn_bk': _L1_xattn_in['bk'], 'L1_xattn_Wv': _L1_xattn_in['Wv'], 'L1_xattn_bv': _L1_xattn_in['bv'], 'L1_xattn_Wo': _L1_xattn_in['Wo'], 'L1_xattn_bo': _L1_xattn_in['bo'], 'L1_xattn_ln_gamma': _L1_xattn_in['ln_gamma'], 'L1_xattn_ln_beta': _L1_xattn_in['ln_beta'], 'L1_xattn_residual_scale': _L1_xattn_in['residual_scale'], 'L1_ffn_W_up': _L1_ffn_in['W_up'], 'L1_ffn_W_down': _L1_ffn_in['W_down'], 'L1_ffn_W_gate': _L1_ffn_in['W_gate'], 'L1_ffn_W_expert': _L1_ffn_in['W_expert']}

def reference(x, ctx_2048, mask_BxS2_ik0, L0_xattn_wq, L0_xattn_bq, L0_xattn_wkv, L0_xattn_bkv, L0_xattn_wp, L0_xattn_bp, L0_ffn_W1, L0_ffn_W2, L1_xattn_Wq, L1_xattn_bq, L1_xattn_Wk, L1_xattn_bk, L1_xattn_Wv, L1_xattn_bv, L1_xattn_Wo, L1_xattn_bo, L1_xattn_ln_gamma, L1_xattn_ln_beta, L1_xattn_residual_scale, L1_ffn_W_up, L1_ffn_W_down, L1_ffn_W_gate, L1_ffn_W_expert):
    import jax
    import jax.numpy as jnp

    def _L0_xattn_ref(x, cond, wq, bq, wkv, bkv, wp, bp):
        import jax, jax.numpy as jnp
        import numpy as np
        NUM_HEADS = 16

        def _qdq(x):
            s = jnp.maximum(jnp.max(jnp.abs(x), axis=-1, keepdims=True) / 127.0, 1e-08)
            return jnp.clip(jnp.round(x / s), -127.0, 127.0) * s
        B, N, C = x.shape
        M = cond.shape[1]
        H = NUM_HEADS
        Dh = C // H
        q = _qdq(x) @ _qdq(wq).T + bq
        kv = cond @ wkv.T + bkv
        k, v = jnp.split(kv, 2, axis=-1)
        q = q.reshape(B, N, H, Dh)
        k = k.reshape(B, M, H, Dh)
        v = v.reshape(B, M, H, Dh)
        scale = 1.0 / np.sqrt(Dh)
        attn = jax.nn.softmax(jnp.einsum('bnhd,bmhd->bhnm', q, k) * scale, axis=-1)
        o = jnp.einsum('bhnm,bmhd->bnhd', attn, v).reshape(B, N, C)
        out = _qdq(o) @ _qdq(wp).T + bp
        return out

    def _L0_ffn_ref(x, W1, W2):
        import jax, jax.numpy as jnp
        import numpy as np
        D_MODEL = 512
        D_FF = 2048
        BATCH = 4
        SEQ = 512
        MAX_EXP = 4
        NUM_BITS = 8
        C_CHUNKS = 2
        SCALE = 0.1

        def _pow2_ternary(key, out_dim, in_dim, max_exp):
            k1, k2 = jax.random.split(key)
            t = jax.random.randint(k1, (out_dim, in_dim), -1, 2).astype(jnp.float32)
            e = jax.random.randint(k2, (out_dim, in_dim), 0, max_exp + 1).astype(jnp.float32)
            return t * jnp.exp2(-e)

        def _lookup_act(h):
            total_bits = NUM_BITS * C_CHUNKS
            qmax = 2 ** (total_bits - 1) - 1
            qmin = -2 ** (total_bits - 1)
            q = jnp.clip(jnp.round(h / SCALE), qmin, qmax)
            return jax.nn.gelu(q * SCALE)
        h = jnp.einsum('bsd,fd->bsf', x, W1)
        a = _lookup_act(h)
        return jnp.einsum('bsf,df->bsd', a, W2)

    def _L1_xattn_ref(hidden_states, audio_tokens, attention_mask, Wq, bq, Wk, bk, Wv, bv, Wo, bo, ln_gamma, ln_beta, residual_scale):
        import jax, jax.numpy as jnp
        import numpy as np
        import math
        H = 512
        NH = 16
        HD = H // NH
        EPS_LN = 1e-05
        RES_SCALE_MAX = 0.3

        def _nan_clean(x, lim=10000.0):
            return jnp.nan_to_num(x, nan=0.0, posinf=lim, neginf=-lim)
        B, S, _ = hidden_states.shape
        T = audio_tokens.shape[1]
        hs = _nan_clean(hidden_states).astype(jnp.float32)
        at = _nan_clean(audio_tokens).astype(jnp.float32)

        def proj(x, W, b, L):
            y = x @ W.T + b
            return y.reshape(B, L, NH, HD).transpose(0, 2, 1, 3)
        q = _nan_clean(proj(hs, Wq, bq, S))
        k = _nan_clean(proj(at, Wk, bk, T))
        v = _nan_clean(proj(at, Wv, bv, T))
        scale = max(math.sqrt(HD), 1e-08)
        scores = jnp.einsum('bhsd,bhtd->bhst', q, k) / scale
        scores = jnp.clip(scores, -50.0, 50.0)
        scores = jnp.nan_to_num(scores, nan=0.0, posinf=50.0, neginf=-50.0)
        attend = (attention_mask.astype(jnp.float32) > 0.5)[:, None, None, :]
        scores = jnp.where(attend, scores, -10000.0)
        scores = jnp.clip(scores, -50.0, 50.0)
        probs = jax.nn.softmax(scores, axis=-1)
        probs = jnp.nan_to_num(probs, nan=0.0, posinf=1.0, neginf=0.0)
        probs = probs / (probs.sum(axis=-1, keepdims=True) + 1e-08)
        ctx = jnp.einsum('bhst,bhtd->bhsd', probs, v)
        ctx = ctx.transpose(0, 2, 1, 3).reshape(B, S, H)
        delta = _nan_clean(ctx @ Wo.T + bo)
        rs = jnp.clip(residual_scale, 0.0, RES_SCALE_MAX)
        delta = rs * delta
        mu = delta.mean(axis=-1, keepdims=True)
        var = jnp.mean((delta - mu) ** 2, axis=-1, keepdims=True)
        delta = (delta - mu) / jnp.sqrt(var + EPS_LN) * ln_gamma + ln_beta
        return delta

    def _L1_ffn_ref(x, W_up, W_down, W_gate, W_expert):
        import jax, jax.numpy as jnp
        import numpy as np
        DIM = 512
        N_EXPERTS = 8
        TOP_K = 2
        logits = jnp.einsum('bsd,ed->bse', x, W_gate)
        routing_weights, selected_experts = jax.lax.top_k(logits, TOP_K)
        shared_out = jnp.einsum('bsd,od->bso', jax.nn.relu(jnp.einsum('bsd,od->bso', x, W_up)), W_down)
        rw = jax.nn.softmax(routing_weights, axis=-1)
        expert_out = jnp.einsum('bsd,do->bso', x, W_expert)
        moe_out = jnp.sum(rw, axis=-1, keepdims=True) * expert_out
        return shared_out + moe_out
    x = x + _L0_xattn_ref(_layernorm(x, axis=-1), ctx_2048, L0_xattn_wq, L0_xattn_bq, L0_xattn_wkv, L0_xattn_bkv, L0_xattn_wp, L0_xattn_bp)
    x = x + _L0_ffn_ref(_layernorm(x, axis=-1), L0_ffn_W1, L0_ffn_W2)
    x = x + _L1_xattn_ref(_layernorm(x, axis=-1), ctx_2048, mask_BxS2_ik0, L1_xattn_Wq, L1_xattn_bq, L1_xattn_Wk, L1_xattn_bk, L1_xattn_Wv, L1_xattn_bv, L1_xattn_Wo, L1_xattn_bo, L1_xattn_ln_gamma, L1_xattn_ln_beta, L1_xattn_residual_scale)
    x = x + _L1_ffn_ref(_layernorm(x, axis=-1), L1_ffn_W_up, L1_ffn_W_down, L1_ffn_W_gate, L1_ffn_W_expert)
    return x

_drawn_inputs = setup_inputs


def setup_inputs(seed=0):
    import zlib

    import numpy as np

    out = dict(_drawn_inputs(seed))
    spreads = {'L1_xattn_bq': (0.0, 2.0),
     'L1_xattn_bk': (0.0, 2.0),
     'L1_xattn_bv': (0.0, 2.0),
     'L1_xattn_bo': (0.0, 2.0),
     'L1_xattn_ln_gamma': (1.0, 0.6),
     'L1_xattn_ln_beta': (0.0, 2.0)}
    factors = {'L0_xattn_wq': 7.094,
     'L0_xattn_bq': 64.0,
     'L0_xattn_bkv': 5.631,
     'L0_xattn_bp': 2.737,
     'L1_xattn_Wq': 64.0,
     'L1_xattn_Wk': 64.0,
     'L1_xattn_Wv': 39.428,
     'L1_xattn_Wo': 36.935,
     'L1_ffn_W_up': 8.0,
     'L1_ffn_W_down': 8.0,
     'L1_ffn_W_gate': 64.0,
     'L1_ffn_W_expert': 7.388}
    for name, (base, spread) in spreads.items():
        noise = np.random.default_rng([zlib.crc32(name.encode()), seed]).standard_normal(out[name].shape)
        drawn = base * np.exp(spread * noise) if base else spread * noise
        out[name] = jnp.asarray(drawn.astype(out[name].dtype))
    for name, factor in factors.items():
        out[name] = (out[name] * factor).astype(out[name].dtype)
    return out
```

```python
from contextlib import ExitStack

import concourse.bass as bass
from concourse import mybir

F32 = mybir.dt.float32
F32R = mybir.dt.float32r
BF16 = mybir.dt.bfloat16
I32 = mybir.dt.int32
ALU = mybir.AluOpType
ACT = mybir.ActivationFunctionType
AX = mybir.AxisListType

P = 128
B, S, D, T, H, FF, NE = 4, 512, 512, 1601, 16, 2048, 8
DH = D // H
KT = D // P
RT = S // P
HPG = P // DH
NG = H // HPG
TT = -(-T // P)
TP = T + T % 2
TROWS = [min(P, T - P * i) for i in range(TT)]
KCH = [(0, 402), (402, 400), (802, 400), (1202, 400)]
MCH, MW, MV = [0, 400, 800, 1200], 402, 401
FT = FF // P
MAGIC = 12582912.0
ROOT = float(DH) ** 0.5
EPS = 1e-5


class Lane:

    def __init__(self, engine, sem):
        self.e, self.sem, self.n, self.seen = engine, sem, 0, {}

    def wait(self, *tokens):
        for t in tokens:
            if t is not None and self.seen.get(id(t[0]), 0) < t[1]:
                self.e.wait_ge(t[0], t[1])
                self.seen[id(t[0])] = t[1]

    def mark(self, instruction):
        instruction.then_inc(self.sem, 1)
        self.n += 1
        return self.sem, self.n


class Core:
    def __init__(self, nc, stack):
        self.nc = nc
        sem = lambda name: stack.enter_context(nc.semaphore(name))
        self.pe = Lane(nc.tensor, sem("pe_done"))
        self.act = Lane(nc.scalar, sem("act_done"))
        self.dve = Lane(nc.vector, sem("dve_done"))
        self.pool = Lane(nc.gpsimd, sem("pool_done"))
        self.sp = Lane(nc.sync, None)
        self.lanes = (self.pe, self.act, self.dve, self.pool, self.sp)
        self.dma_sems = [sem(f"dma_{i}") for i in range(24)]
        self.dma_count = {}

    def dma(self, k, dst, src, *tokens, lane=None):
        lane = lane or self.sp
        lane.wait(*tokens)
        dst, src = (x.bitcast(F32) if x.dtype == F32R else x for x in (dst, src))
        lane.e.dma_start(dst, src).then_inc(self.dma_sems[k], 16)
        self.dma_count[k] = self.dma_count.get(k, 0) + 16
        return self.dma_sems[k], self.dma_count[k]

    def fence(self):
        for k, n in self.dma_count.items():
            self.sp.wait((self.dma_sems[k], n))
        for lane in self.lanes[:4]:
            if lane.n:
                lane.wait((lane.sem, lane.n))
        self.nc.all_engine_barrier()
        for lane in self.lanes[:4]:
            if lane.n:
                lane.e.sem_clear(lane.sem)
        for k in self.dma_count:
            self.sp.e.sem_clear(self.dma_sems[k])
        self.nc.all_engine_barrier()
        for lane in self.lanes:
            lane.n, lane.seen = 0, {}
        self.dma_count = {}


class Ring:

    def __init__(self, buffers):
        self.buffers, self.free, self.at = buffers, [()] * len(buffers), -1

    def next(self):
        self.at = (self.at + 1) % len(self.buffers)
        return self.at, self.buffers[self.at]

    def reset(self):
        self.free, self.at = [()] * len(self.buffers), -1


def at(dram, i):
    if isinstance(i, int):
        return dram[i]
    names = "abcdef"[:len(dram.shape) - 1]
    return dram[bass.ds(i, 1)].rearrange(f"o {' '.join(names)} -> (o {names[0]}) {' '.join(names[1:])}")


def f32(ap):
    return ap.bitcast(F32)


def build(nc, a, out):
    stack = ExitStack()
    with stack:
        core = Core(nc, stack)
        pe, act, dve, pool, sp = core.lanes
        V, A, M, G = nc.vector, nc.scalar, nc.tensor, nc.gpsimd

        psum = stack.enter_context(nc.psum_tensor("psum", [P, 8, 512], F32))
        bank = lambda i: psum[:, i, :]
        banks = Ring([bank(i) for i in range(8)])

        def sbuf(scope, name, shape, dt=F32):
            return scope.enter_context(nc.sbuf_tensor(name, shape, dt))

        ident = sbuf(stack, "ident", [P, P])
        minus_half = sbuf(stack, "minus_half", [P, RT])

        def scratch(name, shape, dt=F32):
            return nc.dram_tensor(name, shape, dt).ap()

        k_hi = [scratch(f"k_hi{n}", (B * NG, P, TP)) for n in range(2)]
        k_lo = [scratch(f"k_lo{n}", (B * NG, P, TP)) for n in range(2)]
        v_rows = [scratch(f"v_rows{n}", (B, TT * P, D)) for n in range(2)]
        q_hi = [scratch(f"q_hi{n}", (B * NG, P, S)) for n in range(2)]
        q_lo = [scratch(f"q_lo{n}", (B * NG, P, S)) for n in range(2)]
        o_t = [scratch(f"o_t{n}", (B * NG, P, S)) for n in range(2)]
        x_mid = [scratch(f"x_mid{n}", (B, S, D)) for n in range(3)]
        x_in = a["x"]

        t0 = pool.mark(G.memset(ident[:], 0.0))
        pool.wait(t0)
        pool.mark(G.affine_select(out=ident[:], in_=ident[:], compare_op=ALU.not_equal, fill=1.0,
                                  base=0, pattern=[[-1, P]], channel_multiplier=1))
        dve.mark(V.memset(minus_half[:], -0.5))
        core.fence()

        def split(hi, lo, src, *tokens):
            act.wait(*tokens)
            h = act.mark(A.activation(hi, src, ACT.Copy))
            dve.wait(h, *tokens)
            return dve.mark(V.tensor_tensor(lo, src, f32(hi), ALU.subtract))

        def load_split_weight(scope, name, dram, stage, width):
            n = dram.shape[0] // P
            hi = sbuf(scope, f"{name}_hi", [P, n, width], F32R)
            lo = sbuf(scope, f"{name}_lo", [P, n, width], F32R)
            done = None
            for k in range(n):
                for c in range(0, width, 512):
                    w = min(512, width - c)
                    i, buf = stage.next()
                    got = core.dma(i, buf[:, 0:w], dram[k * P:(k + 1) * P, c:c + w], *stage.free[i])
                    done = split(hi[:, k, c:c + w], lo[:, k, c:c + w], buf[:, 0:w], got)
                    stage.free[i] = (done,)
            return hi, lo, done

        def products(dst, terms, *tokens):
            pe.wait(*tokens)
            for n, (lhs, rhs) in enumerate(terms):
                m = M.matmul(dst, lhs, rhs, start=(n == 0), stop=(n == len(terms) - 1))
            return pe.mark(m)

        def three(l_hi, l_lo, r_hi, r_lo):
            return [(l_hi, r_hi), (l_hi, r_lo), (l_lo, r_hi)]

        def layer_norm(rows, normed, small, *tokens):
            stats, mv, ve, r, t = small
            dve.wait(*tokens)
            for k in range(RT):
                s = dve.mark(V.bn_stats(stats[:, k, :], rows[:, k, :]))
            dve.wait(s)
            for k in range(RT):
                s = dve.mark(V.bn_aggr(mv[:, k, :], stats[:, k, :]))
            dve.wait(s)
            s = dve.mark(V.tensor_scalar(ve[:], mv[:, :, 1], EPS, None, ALU.add))
            pool.wait(s)
            s = pool.mark(G.tensor_tensor(r[:], ve[:], minus_half[:], ALU.pow))
            dve.wait(s)
            s = dve.mark(V.tensor_tensor(t[:], r[:], r[:], ALU.mult))
            dve.wait(s)
            s = dve.mark(V.tensor_tensor(t[:], t[:], ve[:], ALU.mult))
            dve.wait(s)
            s = dve.mark(V.tensor_scalar(t[:], t[:], -0.5, 1.5, ALU.mult, ALU.add))
            dve.wait(s)
            s = dve.mark(V.tensor_tensor(r[:], r[:], t[:], ALU.mult))
            dve.wait(s)
            for k in range(RT):
                s = dve.mark(V.tensor_scalar(normed[:, k, :], rows[:, k, :], mv[:, k, 0:1], r[:, k:k + 1],
                                             ALU.subtract, ALU.mult))
            return s

        def norm_small(scope, tag):
            return (sbuf(scope, f"stats_{tag}", [P, RT, 6]), sbuf(scope, f"mv_{tag}", [P, RT, 2]),
                    sbuf(scope, f"ve_{tag}", [P, RT]), sbuf(scope, f"r_{tag}", [P, RT]),
                    sbuf(scope, f"t_{tag}", [P, RT]))

        def quantise(rows, scale, recip, *tokens):
            dve.wait(*tokens)
            s = dve.mark(V.tensor_reduce(scale[:], rows[:], AX.X, ALU.max, apply_absolute_value=True))
            dve.wait(s)
            s = dve.mark(V.tensor_scalar(scale[:], scale[:], 1.0 / 127.0, 1e-8, ALU.mult, ALU.max))
            dve.wait(s)
            s = dve.mark(V.reciprocal(recip[:], scale[:]))
            dve.wait(s)
            for k in range(RT):
                s = dve.mark(V.tensor_scalar(rows[:, k, :], rows[:, k, :], recip[:, k:k + 1], 127.0,
                                             ALU.mult, ALU.min))
            dve.wait(s)
            s = dve.mark(V.tensor_scalar(rows[:], rows[:], -127.0, MAGIC, ALU.max, ALU.add))
            dve.wait(s)
            return dve.mark(V.tensor_scalar(rows[:], rows[:], MAGIC, None, ALU.subtract))

        def transposed(rows, use, *tokens):
            for k in range(KT):
                i, dst = banks.next()
                pe.wait(*banks.free[i], *tokens)
                for r in range(RT):
                    m = M.transpose(dst[:, r * P:(r + 1) * P], rows[:, r, k * P:(k + 1) * P], ident[:])
                banks.free[i] = (use(k, dst, pe.mark(m)),)
            return banks.free[i][0]

        def load_rows(k, dst, dram, i, *tokens):
            return core.dma(k, dst[:], at(dram, i).rearrange("(r p) d -> p r d", p=P), *tokens)

        def store_rows(k, dram, i, src, *tokens):
            return core.dma(k, at(dram, i).rearrange("(r p) d -> p r d", p=P), src[:], *tokens)

        def quantised_weight(scope, name, dram, stage_rows):
            wt = sbuf(scope, f"{name}_t", [P, KT, D], BF16)
            scale = sbuf(scope, f"{name}_scale", [P, KT])
            recip = sbuf(scope, f"{name}_recip", [P, KT])
            got = core.dma(0, stage_rows[:], dram.rearrange("(r p) d -> p r d", p=P))
            q = quantise(stage_rows, scale, recip, got)

            def keep(k, src, token):
                act.wait(token)
                return act.mark(A.activation(wt[:, k, :], src, ACT.Copy))
            return wt, scale, transposed(stage_rows, keep, q)

        def row_of(dst, columns, *tokens):
            i, ps = banks.next()
            pe.wait(*banks.free[i], *tokens)
            for r in range(RT):
                m = M.matmul(ps[:, r * P:(r + 1) * P], columns[:, r:r + 1].to_broadcast([P, P]), ident[:],
                             start=True, stop=True)
            token = pe.mark(m)
            act.wait(token)
            banks.free[i] = (act.mark(A.activation(dst, ps, ACT.Copy)),)
            return banks.free[i][0]

        def start_loop():
            core.fence()
            banks.reset()

        def end_loop():
            core.fence()
            banks.reset()

        def kv_projection():
            with ExitStack() as scope:
                stage = Ring([sbuf(scope, f"kv_stage{i}", [P, 512]) for i in range(4)])
                wk, wv, bk, bv = [], [], [], []
                for n, (kd, vd) in enumerate(((a["wkv0_t"][:, 0:D], a["wkv0_t"][:, D:2 * D]),
                                              (a["wk1_t"], a["wv1_t"]))):
                    wk.append(load_split_weight(scope, f"wk{n}", kd, stage, D))
                    wv.append(load_split_weight(scope, f"wv{n}", vd, stage, D))
                    bk.append(sbuf(scope, f"bk{n}", [P, KT]))
                    bv.append(sbuf(scope, f"bv{n}", [P, D]))
                    core.dma(4, bk[n][:], a[f"bk{n}"])
                    core.dma(4, bv[n][:], a[f"bv{n}"].partition_broadcast(P))
                raw = [sbuf(scope, f"ctx_raw{k}", [P, T]) for k in range(2)]
                c_hi = sbuf(scope, "ctx_hi", [P, KT, TP], F32R)
                c_lo = sbuf(scope, "ctx_lo", [P, KT, TP], F32R)
                kt_hi = [sbuf(scope, f"kt_hi{i}", [P, TP], F32R) for i in range(2)]
                kt_lo = [sbuf(scope, f"kt_lo{i}", [P, TP], F32R) for i in range(2)]
                v_out = [sbuf(scope, f"v_out{i}", [P, D]) for i in range(4)]
                dve.mark(V.memset(f32(c_hi[:, :, T:TP]), 0.0))
                dve.mark(V.memset(f32(c_lo[:, :, T:TP]), 0.0))
                start_loop()
                with nc.Fori(0, B) as b:
                    ready = None
                    raw_free = [(), ()]
                    src = at(a["ctx_t"], b)
                    for k in range(KT):
                        got = core.dma(k, raw[k % 2][:], src[k * P:(k + 1) * P, :], *raw_free[k % 2])
                        ready = split(c_hi[:, k, 0:T], c_lo[:, k, 0:T], raw[k % 2][:], got)
                        raw_free[k % 2] = (ready,)
                    kt_free = [(), ()]
                    v_free = [()] * 4
                    nk = nv = 0
                    for n in range(2):
                        w_hi, w_lo, _ = wk[n]
                        for g in range(NG):
                            s = nk % 2
                            nk += 1
                            for c0, cw in KCH:
                                i, ps = banks.next()
                                terms = []
                                for k in range(KT):
                                    terms += three(w_hi[:, k, g * P:(g + 1) * P], w_lo[:, k, g * P:(g + 1) * P],
                                                   c_hi[:, k, c0:c0 + cw], c_lo[:, k, c0:c0 + cw])
                                done = products(ps[:, 0:cw], terms, ready, *banks.free[i])
                                act.wait(done, *kt_free[s])
                                h = act.mark(A.activation(kt_hi[s][:, c0:c0 + cw], ps[:, 0:cw], ACT.Identity,
                                                          bias=bk[n][:, g:g + 1]))
                                dve.wait(h, *kt_free[s])
                                banks.free[i] = (dve.mark(V.scalar_tensor_tensor(
                                    out=kt_lo[s][:, c0:c0 + cw], in0=ps[:, 0:cw], scalar=bk[n][:, g:g + 1],
                                    in1=f32(kt_hi[s][:, c0:c0 + cw]), op0=ALU.add, op1=ALU.subtract)),)
                            core.dma(4 + s, at(k_hi[n], b * NG + g), kt_hi[s][:], h)
                            kt_free[s] = (core.dma(4 + s, at(k_lo[n], b * NG + g), kt_lo[s][:],
                                                   *banks.free[i]),)
                        w_hi, w_lo, _ = wv[n]
                        for t, rows in enumerate(TROWS):
                            s = nv % 4
                            nv += 1
                            i, ps = banks.next()
                            terms = []
                            for k in range(KT):
                                terms += three(c_hi[:, k, t * P:t * P + rows], c_lo[:, k, t * P:t * P + rows],
                                               w_hi[:, k, :], w_lo[:, k, :])
                            done = products(ps[0:rows, :], terms, ready, *banks.free[i])
                            dve.wait(done, *v_free[s])
                            banks.free[i] = (dve.mark(V.tensor_tensor(v_out[s][0:rows, :], ps[0:rows, :],
                                                                      bv[n][0:rows, :], ALU.add)),)
                            v_free[s] = (core.dma(6 + s, at(v_rows[n], b)[t * P:t * P + rows, :],
                                                  v_out[s][0:rows, :], *banks.free[i]),)
                    end_loop()

        def store_q(n, b, g, parts, token, s):
            core.dma(8 + s, at(q_hi[n], b * NG + g), parts[0][:], token)
            return core.dma(8 + s, at(q_lo[n], b * NG + g), parts[1][:], token)

        def q_projection_0():
            with ExitStack() as scope:
                rows = sbuf(scope, "q0_rows", [P, RT, D])
                normed = sbuf(scope, "q0_normed", [P, RT, D])
                small = norm_small(scope, "q0")
                step = sbuf(scope, "q0_step", [P, RT])
                recip = sbuf(scope, "q0_recip", [P, RT])
                step_row = sbuf(scope, "q0_step_row", [P, S])
                xq_t = sbuf(scope, "q0_xq_t", [P, KT, S], BF16)
                bq = sbuf(scope, "q0_bq", [P, KT])
                full = [sbuf(scope, f"q0_full{i}", [P, S]) for i in range(2)]
                parts = [[sbuf(scope, f"q0_part{i}{j}", [P, S], F32R) for j in range(2)] for i in range(2)]
                wt, w_step, _ = quantised_weight(scope, "wq0", a["wq0"], rows)
                core.dma(1, bq[:], a["bq0"])
                start_loop()
                with nc.Fori(0, B) as b:
                    got = load_rows(0, rows, x_in, b)
                    s = layer_norm(rows, normed, small, got)
                    s = quantise(normed, step, recip, s)
                    stepped = row_of(step_row[:], step, s)

                    def keep(k, src, token):
                        act.wait(token)
                        return act.mark(A.activation(xq_t[:, k, :], src, ACT.Copy))
                    ready = transposed(normed, keep, s)
                    free = [(), ()]
                    for g in range(NG):
                        i, ps = banks.next()
                        done = products(ps, [(wt[:, k, g * P:(g + 1) * P], xq_t[:, k, :]) for k in range(KT)],
                                        ready, *banks.free[i])
                        f, (hi, lo) = full[g % 2], parts[g % 2]
                        dve.wait(done, stepped, *free[g % 2])
                        t = dve.mark(V.scalar_tensor_tensor(out=f[:], in0=ps, scalar=w_step[:, g:g + 1],
                                                            in1=step_row[:], op0=ALU.mult, op1=ALU.mult))
                        banks.free[i] = (t,)
                        dve.wait(t)
                        h = dve.mark(V.tensor_scalar(hi[:], f[:], bq[:, g:g + 1], None, ALU.add))
                        dve.wait(h)
                        l = dve.mark(V.scalar_tensor_tensor(out=lo[:], in0=f[:], scalar=bq[:, g:g + 1],
                                                            in1=f32(hi[:]), op0=ALU.add, op1=ALU.subtract))
                        free[g % 2] = (store_q(0, b, g, (hi, lo), l, g % 2),)
                    end_loop()

        def q_projection_1():
            with ExitStack() as scope:
                rows = sbuf(scope, "q1_rows", [P, RT, D])
                normed = sbuf(scope, "q1_normed", [P, RT, D])
                small = norm_small(scope, "q1")
                x_hi = sbuf(scope, "q1_x_hi", [P, KT, S], F32R)
                x_lo = sbuf(scope, "q1_x_lo", [P, KT, S], F32R)
                bq = sbuf(scope, "q1_bq", [P, KT])
                parts = [[sbuf(scope, f"q1_part{i}{j}", [P, S], F32R) for j in range(2)] for i in range(2)]
                stage = Ring([sbuf(scope, f"q1_stage{i}", [P, 512]) for i in range(4)])
                w_hi, w_lo, _ = load_split_weight(scope, "wq1", a["wq1_t"], stage, D)
                core.dma(5, bq[:], a["bq1"])
                start_loop()
                with nc.Fori(0, B) as b:
                    got = load_rows(0, rows, x_mid[1], b)
                    s = layer_norm(rows, normed, small, got)
                    ready = transposed(normed, lambda k, src, t: split(x_hi[:, k, :], x_lo[:, k, :], src, t), s)
                    free = [(), ()]
                    for g in range(NG):
                        i, ps = banks.next()
                        terms = []
                        for k in range(KT):
                            terms += three(w_hi[:, k, g * P:(g + 1) * P], w_lo[:, k, g * P:(g + 1) * P],
                                           x_hi[:, k, :], x_lo[:, k, :])
                        done = products(ps, terms, ready, *banks.free[i])
                        hi, lo = parts[g % 2]
                        act.wait(done, *free[g % 2])
                        h = act.mark(A.activation(hi[:], ps, ACT.Identity, bias=bq[:, g:g + 1]))
                        dve.wait(h, *free[g % 2])
                        l = dve.mark(V.scalar_tensor_tensor(out=lo[:], in0=ps, scalar=bq[:, g:g + 1],
                                                            in1=f32(hi[:]), op0=ALU.add, op1=ALU.subtract))
                        banks.free[i] = (l,)
                        free[g % 2] = (store_q(1, b, g, (hi, lo), l, g % 2),)
                    end_loop()

        def attention(n):
            first = n == 0
            NQ = 3 if first else 4
            with ExitStack() as scope:
                k_st = [sbuf(scope, f"k_st{n}{s}", [P, HPG, TP], F32R) for s in range(NG)]
                q_st = [sbuf(scope, f"q_st{n}{s}", [P, HPG, S], F32R) for s in range(NG)]
                v_st = [sbuf(scope, f"v_st{n}{s}", [P, TT, P]) for s in range(NG)]
                probs = Ring([sbuf(scope, f"probs{n}{i}", [P, HPG, S]) for i in range(2)])
                ones = sbuf(scope, f"ones{n}", [P, DH])
                acc_sb = sbuf(scope, f"acc_sb{n}", [P, S])
                den_sb = sbuf(scope, f"den_sb{n}", [P, S])
                rec = sbuf(scope, f"rec{n}", [P, S])
                o_sb = sbuf(scope, f"o_sb{n}", [P, S])
                scores = Ring([psum[:, 0:2, :], psum[:, 2:4, :]])
                small_banks = Ring([bank(4), bank(5)])
                acc, den = bank(6), bank(7)
                dve.mark(V.memset(ones[:], 1.0))
                if first:
                    neg_max = sbuf(scope, "neg_max", [P, HPG, RT, DH])
                    win_max = sbuf(scope, "win_max", [P, HPG, RT, 4])
                    max_hi = sbuf(scope, "max_hi", [P, HPG, RT], F32R)
                    dve.mark(V.memset(neg_max[:], 0.0))
                    for s in range(NG):
                        dve.mark(V.memset(f32(k_st[s][96:128, :, :]), 1.0))
                else:
                    mask_i = sbuf(scope, "mask_i", [P, B, TT], I32)
                    bound = sbuf(scope, "bound", [P, B, TT])
                    top = sbuf(scope, "top", [P, TT])
                    got = core.dma(9, mask_i[:], a["mask_t"])
                    dve.wait(got)
                    s_ = dve.mark(V.tensor_scalar(bound[:], mask_i[:], 0.5, 100.0 * ROOT, ALU.is_gt, ALU.mult))
                    dve.wait(s_)
                    dve.mark(V.tensor_scalar(bound[:], bound[:], 50.0 * ROOT, None, ALU.subtract))

                loaded = {}

                def load(s, unit, b, g, *tokens):
                    for quarter in range(NQ):
                        rows = slice(quarter * DH, (quarter + 1) * DH)
                        k_src = (k_hi, k_lo, k_hi, k_lo)[quarter][n]
                        q_src = (q_hi, q_hi, q_lo, q_lo)[quarter][n]
                        core.dma(s, k_st[s][rows, :, :], at(k_src, unit).rearrange("(j d) t -> d j t", d=DH),
                                 *tokens)
                        core.dma(s, q_st[s][rows, :, :], at(q_src, unit).rearrange("(j d) t -> d j t", d=DH))
                    v_src = at(v_rows[n], b)[:, g * P:(g + 1) * P]
                    core.dma(s, v_st[s][:, 0:TT - 1, :],
                             v_src[0:(TT - 1) * P, :].rearrange("(t p) c -> p t c", p=P))
                    loaded[s] = core.dma(s, v_st[s][0:TROWS[-1], TT - 1, :], v_src[(TT - 1) * P:T, :])

                def max_pass(s):
                    pieces, done = [], {}

                    def window(j, r, c):
                        i, ps = small_banks.next()
                        pe.wait(loaded.get(s), *small_banks.free[i])
                        m = pe.mark(M.matmul(ps[:, 0:MW], q_st[s][0:96, j, r * P:(r + 1) * P],
                                             k_st[s][0:96, j, MCH[c]:MCH[c] + MW], start=True, stop=True))
                        dve.wait(m)
                        done[j] = dve.mark(V.tensor_reduce(win_max[:, j, r, c:c + 1], ps[:, 0:MV], AX.X, ALU.max))
                        small_banks.free[i] = (done[j],)

                    def columns(j):
                        dve.wait(done[j])
                        t = dve.mark(V.tensor_reduce(neg_max[:, j, :, 0], win_max[:, j, :, :], AX.X, ALU.max,
                                                     negate=True))
                        dve.wait(t)
                        t = dve.mark(V.tensor_copy(max_hi[:, j, :], neg_max[:, j, :, 0]))
                        dve.wait(t)
                        done[j] = dve.mark(V.tensor_tensor(neg_max[:, j, :, 1], neg_max[:, j, :, 0],
                                                           f32(max_hi[:, j, :]), ALU.subtract))

                    def turn(j):
                        i, ps = small_banks.next()
                        pe.wait(done[j], *small_banks.free[i])
                        for r in range(RT):
                            m = M.matmul(ps[96:128, r * P:(r + 1) * P], neg_max[:, j, r, :], ident[:],
                                         start=True, stop=True)
                        t = pe.mark(m)
                        dve.wait(t)
                        max_ready[s] = dve.mark(V.tensor_copy(q_st[s][96:128, j, :], ps[96:128, :]))
                        small_banks.free[i] = (max_ready[s],)

                    for j in range(HPG):
                        for r in range(RT):
                            for c in range(4):
                                pieces.append(lambda j=j, r=r, c=c: window(j, r, c))
                                if j and r == 0 and c == 2:
                                    pieces.append(lambda j=j: turn(j - 1))
                        pieces.append(lambda j=j: columns(j))
                    pieces.append(lambda: None)
                    pieces.append(lambda: turn(HPG - 1))
                    return pieces

                max_ready = {}
                state = {}

                def attend(s, unit, b, pieces, spread):
                    todo = list(pieces)
                    tiles = {}

                    def score_tile(t):
                        rows = TROWS[t]
                        pi, pr = probs.next()
                        done = []
                        for pair in range(2):
                            i, ps = scores.next()
                            pe.wait(loaded.get(s), max_ready.get(s), *scores.free[i])
                            for jj in range(2):
                                j = 2 * pair + jj
                                m = M.matmul(ps[0:rows, jj, :], k_st[s][:, j, t * P:t * P + rows],
                                             q_st[s][:, j, :], start=True, stop=True)
                            m = pe.mark(m)
                            dst = pr[0:rows, 2 * pair:2 * pair + 2, :]
                            if first:
                                act.wait(m, *probs.free[pi])
                                e = act.mark(A.activation(dst, ps[0:rows], ACT.Exp, scale=1.0 / ROOT))
                                scores.free[i] = (e,)
                            else:
                                dve.wait(m, *probs.free[pi])
                                c = dve.mark(V.tensor_scalar(dst, ps[0:rows], top[0:rows, t:t + 1], -50.0 * ROOT,
                                                             ALU.min, ALU.max))
                                scores.free[i] = (c,)
                                act.wait(c)
                                e = act.mark(A.activation(dst, dst, ACT.Exp, scale=1.0 / ROOT))
                            done.append(e)
                        tiles[t] = (pi, pr, done)

                    def value_tile(t):
                        rows = TROWS[t]
                        pi, pr, done = tiles.pop(t)
                        pe.wait(*done)
                        if t == 0:
                            pe.wait(*state.get("acc_free", ()))
                        for dst, weights in ((acc, None), (den, ones)):
                            for j in range(HPG):
                                w = v_st[s][0:rows, t, j * DH:(j + 1) * DH] if weights is None else ones[0:rows, :]
                                m = M.matmul(dst[j * DH:(j + 1) * DH, :], w, pr[0:rows, j, :],
                                             start=(t == 0), stop=(t == TT - 1))
                        probs.free[pi] = (pe.mark(m),)
                        return probs.free[pi][0]

                    for t in range(TT + 1):
                        if t < TT:
                            score_tile(t)
                        quota = -(-len(todo) // max(1, TT - t)) if t >= spread else 0
                        half = quota // 2
                        for _ in range(min(half, len(todo))):
                            todo.pop(0)()
                        if t:
                            last = value_tile(t - 1)
                        for _ in range(min(quota - half, len(todo))):
                            todo.pop(0)()
                    act.wait(last, *state.get("sb_free", ()))
                    d = act.mark(A.activation(den_sb[:], den, ACT.Copy))
                    c = act.mark(A.activation(acc_sb[:], acc, ACT.Copy))
                    state["acc_free"] = (c,)
                    dve.wait(d, *state.get("sb_free", ()))
                    r = dve.mark(V.reciprocal(rec[:], den_sb[:]))
                    if not first:
                        dve.wait(r)
                        u = dve.mark(V.scalar_tensor_tensor(out=den_sb[:], in0=den_sb[:], scalar=-1.0, in1=rec[:],
                                                            op0=ALU.mult, op1=ALU.mult))
                        dve.wait(u)
                        r = dve.mark(V.scalar_tensor_tensor(out=rec[:], in0=den_sb[:], scalar=2.0 - 1e-8,
                                                            in1=rec[:], op0=ALU.add, op1=ALU.mult))
                    dve.wait(r, c, *state.get("o_free", ()))
                    o = dve.mark(V.tensor_tensor(o_sb[:], acc_sb[:], rec[:], ALU.mult))
                    state["sb_free"] = (o,)
                    state["o_free"] = (core.dma(8, at(o_t[n], unit), o_sb[:], o, lane=act if False else None),)
                    return last

                def run_all(pieces):
                    for p in pieces:
                        p()

                def batch(b, more):
                    if not first:
                        top_ready = dve.mark(V.tensor_copy(top[:], bound[:, b, :] if isinstance(b, int) else
                                                           bound[:, bass.ds(b, 1), :].rearrange("p o t -> p (o t)")))
                        dve.wait(top_ready)
                    done = {}
                    for g in range(NG):
                        ahead = g + 2
                        if ahead < NG or more:
                            nb = b if ahead < NG else b + 1
                            load(ahead % NG, nb * NG + ahead % NG, nb, ahead % NG,
                                 *((done[ahead - NG],) if ahead >= NG else ()))
                        nxt = (g + 1) % NG
                        pieces = max_pass(nxt) if first and (g + 1 < NG or more) else []
                        done[g] = attend(g, b * NG + g, b, pieces, 0)

                def reset():
                    core.fence()
                    for ring in (probs, scores, small_banks):
                        ring.reset()
                    loaded.clear()
                    max_ready.clear()
                    state.clear()

                load(0, 0, 0, 0)
                load(1, 1, 0, 1)
                if first:
                    pe.wait((dve.sem, dve.n))
                    run_all(max_pass(0))
                reset()
                with nc.Fori(0, B - 1) as b:
                    batch(b, True)
                    reset()
                batch(B - 1, False)
                reset()
                banks.reset()

        def out_projection_0():
            with ExitStack() as scope:
                o_cols = sbuf(scope, "o0_cols", [P, KT, S])
                o_rows = sbuf(scope, "o0_rows", [P, RT, D])
                rows = sbuf(scope, "o0_x", [P, RT, D])
                step = sbuf(scope, "o0_step", [P, RT])
                recip = sbuf(scope, "o0_recip", [P, RT])
                oq_t = sbuf(scope, "o0_oq_t", [P, KT, S], BF16)
                w_row = sbuf(scope, "o0_w_row", [P, D])
                bp = sbuf(scope, "o0_bp", [P, D])
                y = sbuf(scope, "o0_y", [P, RT, D])
                wt, w_step, _ = quantised_weight(scope, "wp0", a["wp0"], o_rows)
                row_of(w_row[:], w_step, (dve.sem, dve.n))
                core.dma(1, bp[:], a["bp0"].partition_broadcast(P))
                start_loop()
                with nc.Fori(0, B) as b:
                    for g in range(NG):
                        got = core.dma(0, o_cols[:, g, :], at(o_t[0], b * NG + g))
                    got_x = load_rows(1, rows, x_in, b)

                    def keep_rows(k, src, token):
                        act.wait(token)
                        return act.mark(A.activation(o_rows[:, k, :], src, ACT.Copy))
                    s = transposed(o_cols, keep_rows, got)
                    s = quantise(o_rows, step, recip, s)

                    def keep(k, src, token):
                        act.wait(token)
                        return act.mark(A.activation(oq_t[:, k, :], src, ACT.Copy))
                    ready = transposed(o_rows, keep, s)
                    for r in range(RT):
                        i, ps = banks.next()
                        done = products(ps, [(oq_t[:, k, r * P:(r + 1) * P], wt[:, k, :]) for k in range(KT)],
                                        ready, *banks.free[i])
                        dve.wait(done)
                        t = dve.mark(V.scalar_tensor_tensor(out=y[:, r, :], in0=ps, scalar=step[:, r:r + 1],
                                                            in1=w_row[:], op0=ALU.mult, op1=ALU.mult))
                        banks.free[i] = (t,)
                        dve.wait(t, got_x)
                        t = dve.mark(V.tensor_tensor(y[:, r, :], y[:, r, :], bp[:], ALU.add))
                        dve.wait(t)
                        t = dve.mark(V.tensor_tensor(rows[:, r, :], rows[:, r, :], y[:, r, :], ALU.add))
                    store_rows(2, x_mid[0], b, rows, t)
                    end_loop()

        def ffn_0():
            with ExitStack() as scope:
                stage = Ring([sbuf(scope, f"f0_stage{i}", [P, 512]) for i in range(2)])
                w1_hi, w1_lo, _ = load_split_weight(scope, "w1", a["w1_t"], stage, FF)
                w2_hi, w2_lo, _ = load_split_weight(scope, "w2", a["w2_t"], stage, D)
                rows = sbuf(scope, "f0_rows", [P, RT, D])
                normed = sbuf(scope, "f0_normed", [P, RT, D])
                small = norm_small(scope, "f0")
                x_hi = sbuf(scope, "f0_x_hi", [P, KT, S], F32R)
                x_lo = sbuf(scope, "f0_x_lo", [P, KT, S], F32R)
                code = [normed[:, 0, :], normed[:, 1, :]]
                gelu = [normed[:, 2, :], normed[:, 3, :]]
                g_hi = [sbuf(scope, f"f0_g_hi{i}", [P, S], F32R) for i in range(2)]
                g_lo = [sbuf(scope, f"f0_g_lo{i}", [P, S], F32R) for i in range(2)]
                hidden = Ring([bank(i) for i in range(4)])
                start_loop()
                with nc.Fori(0, B) as b:
                    got = load_rows(0, rows, x_mid[0], b)
                    s = layer_norm(rows, normed, small, got)
                    ready = transposed(normed, lambda k, src, t: split(x_hi[:, k, :], x_lo[:, k, :], src, t), s)
                    hidden.reset()
                    freed = {}
                    made = {}

                    def first_half(f):
                        i, ps = hidden.next()
                        terms = []
                        for k in range(KT):
                            terms += three(w1_hi[:, k, f * P:(f + 1) * P], w1_lo[:, k, f * P:(f + 1) * P],
                                           x_hi[:, k, :], x_lo[:, k, :])
                        done = products(ps, terms, ready, *hidden.free[i])
                        q, ge = code[f % 2], gelu[f % 2]
                        dve.wait(done, *freed.get(f - 2, ()))
                        t = dve.mark(V.tensor_scalar(q, ps, 10.0, -32768.0, ALU.mult, ALU.max))
                        hidden.free[i] = (t,)
                        dve.wait(t)
                        t = dve.mark(V.tensor_scalar(q, q, 32767.0, MAGIC, ALU.min, ALU.add))
                        dve.wait(t)
                        t = dve.mark(V.tensor_scalar(q, q, MAGIC, 0.1, ALU.subtract, ALU.mult))
                        act.wait(t, *freed.get(f - 2, ()))
                        t = act.mark(A.activation(ge, q, ACT.Gelu_apprx_tanh))
                        made[f] = split(g_hi[f % 2][:], g_lo[f % 2][:], ge, t, *freed.get(f - 2, ()))

                    def second_half(f):
                        pe.wait(made[f])
                        if f == 0:
                            pe.wait(ready)
                        for r in range(RT):
                            terms = three(g_hi[f % 2][:, r * P:(r + 1) * P], g_lo[f % 2][:, r * P:(r + 1) * P],
                                          w2_hi[:, f, :], w2_lo[:, f, :])
                            for m_, (lhs, rhs) in enumerate(terms):
                                m = M.matmul(bank(4 + r), lhs, rhs, start=(f == 0 and m_ == 0),
                                             stop=(f == FT - 1 and m_ == 2))
                        freed[f] = (pe.mark(m),)

                    dve.wait(ready)
                    act.wait(ready)
                    pe.wait(ready)
                    first_half(0)
                    for f in range(FT):
                        if f + 1 < FT:
                            first_half(f + 1)
                        second_half(f)
                    dve.wait(*freed[FT - 1])
                    for r in range(RT):
                        t = dve.mark(V.tensor_tensor(rows[:, r, :], bank(4 + r), rows[:, r, :], ALU.add))
                    store_rows(1, x_mid[1], b, rows, t)
                    end_loop()

        def out_projection_1():
            with ExitStack() as scope:
                stage = Ring([sbuf(scope, f"o1_stage{i}", [P, 512]) for i in range(4)])
                w_hi, w_lo, _ = load_split_weight(scope, "wo1", a["wo1_t"], stage, D)
                o_cols = sbuf(scope, "o1_cols", [P, KT, S])
                o_hi = sbuf(scope, "o1_hi", [P, KT, S], F32R)
                o_lo = sbuf(scope, "o1_lo", [P, KT, S], F32R)
                rows = sbuf(scope, "o1_x", [P, RT, D])
                delta = sbuf(scope, "o1_delta", [P, RT, D])
                normed = sbuf(scope, "o1_normed", [P, RT, D])
                small = norm_small(scope, "o1")
                bo = sbuf(scope, "o1_bo", [P, D])
                gamma = sbuf(scope, "o1_gamma", [P, D])
                beta = sbuf(scope, "o1_beta", [P, D])
                rs = sbuf(scope, "o1_rs", [P, 1])
                core.dma(5, bo[:], a["bo1"].partition_broadcast(P))
                core.dma(5, gamma[:], a["gamma"].partition_broadcast(P))
                core.dma(5, beta[:], a["beta"].partition_broadcast(P))
                got = core.dma(5, rs[:], a["rs"].partition_broadcast(P))
                dve.wait(got)
                dve.mark(V.tensor_scalar(rs[:], rs[:], 0.0, 0.3, ALU.max, ALU.min))
                start_loop()
                with nc.Fori(0, B) as b:
                    got_x = load_rows(1, rows, x_mid[1], b)
                    for g in range(NG):
                        got = core.dma(2 + g, o_cols[:, g, :], at(o_t[1], b * NG + g))
                        ready = split(o_hi[:, g, :], o_lo[:, g, :], o_cols[:, g, :], got)
                    for r in range(RT):
                        i, ps = banks.next()
                        terms = []
                        for k in range(KT):
                            terms += three(o_hi[:, k, r * P:(r + 1) * P], o_lo[:, k, r * P:(r + 1) * P],
                                           w_hi[:, k, :], w_lo[:, k, :])
                        done = products(ps, terms, ready, *banks.free[i])
                        dve.wait(done)
                        t = dve.mark(V.tensor_tensor(delta[:, r, :], ps, bo[:], ALU.add))
                        banks.free[i] = (t,)
                        dve.wait(t)
                        t = dve.mark(V.tensor_scalar(delta[:, r, :], delta[:, r, :], rs[:, 0:1], None, ALU.mult))
                    s = layer_norm(delta, normed, small, t)
                    dve.wait(s, got_x)
                    for r in range(RT):
                        t = dve.mark(V.tensor_tensor(normed[:, r, :], normed[:, r, :], gamma[:], ALU.mult))
                        u = dve.mark(V.tensor_tensor(rows[:, r, :], rows[:, r, :], beta[:], ALU.add))
                    dve.wait(u)
                    t = dve.mark(V.tensor_tensor(rows[:], rows[:], normed[:], ALU.add))
                    store_rows(6, x_mid[2], b, rows, t)
                    end_loop()

        def ffn_1():
            with ExitStack() as scope:
                stage = Ring([sbuf(scope, f"f1_stage{i}", [P, 512]) for i in range(2)])
                wu_hi, wu_lo, _ = load_split_weight(scope, "wu", a["wu_t"], stage, D)
                wd_hi, wd_lo, _ = load_split_weight(scope, "wd", a["wd_t"], stage, D)
                we_hi, we_lo, _ = load_split_weight(scope, "we", a["we"], stage, D)
                wg_hi, wg_lo, _ = load_split_weight(scope, "wg", a["wg_t"], stage, NE)
                rows = sbuf(scope, "f1_rows", [P, RT, D])
                normed = sbuf(scope, "f1_normed", [P, RT, D])
                small = norm_small(scope, "f1")
                x_hi = sbuf(scope, "f1_x_hi", [P, KT, S], F32R)
                x_lo = sbuf(scope, "f1_x_lo", [P, KT, S], F32R)
                h_hi = sbuf(scope, "f1_h_hi", [P, KT, S], F32R)
                h_lo = sbuf(scope, "f1_h_lo", [P, KT, S], F32R)
                logits = sbuf(scope, "f1_logits", [P, RT, NE])
                top = sbuf(scope, "f1_top", [P, RT, NE])
                e2 = sbuf(scope, "f1_e2", [P, RT, 2])
                total = sbuf(scope, "f1_total", [P, RT])
                inverse = sbuf(scope, "f1_inverse", [P, RT])
                weight = sbuf(scope, "f1_weight", [P, RT])
                start_loop()
                with nc.Fori(0, B) as b:
                    got = load_rows(0, rows, x_mid[2], b)
                    s = layer_norm(rows, normed, small, got)
                    ready = transposed(normed, lambda k, src, t: split(x_hi[:, k, :], x_lo[:, k, :], src, t), s)
                    for f in range(KT):
                        i, ps = banks.next()
                        terms = []
                        for k in range(KT):
                            terms += three(wu_hi[:, k, f * P:(f + 1) * P], wu_lo[:, k, f * P:(f + 1) * P],
                                           x_hi[:, k, :], x_lo[:, k, :])
                        done = products(ps, terms, ready, *banks.free[i])
                        act.wait(done)
                        h = act.mark(A.activation(h_hi[:, f, :], ps, ACT.Relu))
                        dve.wait(h)
                        hidden = dve.mark(V.scalar_tensor_tensor(out=h_lo[:, f, :], in0=ps, scalar=0.0,
                                                                 in1=f32(h_hi[:, f, :]), op0=ALU.max,
                                                                 op1=ALU.subtract))
                        banks.free[i] = (hidden,)
                    for r in range(RT):
                        i, ps = banks.next()
                        terms = []
                        for k in range(KT):
                            terms += three(x_hi[:, k, r * P:(r + 1) * P], x_lo[:, k, r * P:(r + 1) * P],
                                           wg_hi[:, k, :], wg_lo[:, k, :])
                        done = products(ps[:, 0:NE], terms, *banks.free[i])
                        dve.wait(done)
                        t = dve.mark(V.tensor_copy(logits[:, r, :], ps[:, 0:NE]))
                        banks.free[i] = (t,)
                        dve.wait(t)
                        t = dve.mark(V.max(top[:, r, :], logits[:, r, :]))
                    dve.wait(t)
                    for r in range(RT):
                        t = dve.mark(V.tensor_scalar(e2[:, r, :], top[:, r, 0:2], top[:, r, 0:1], None, ALU.subtract))
                    act.wait(t)
                    t = act.mark(A.activation(e2[:], e2[:], ACT.Exp))
                    dve.wait(t)
                    t = dve.mark(V.tensor_reduce(total[:], e2[:], AX.X, ALU.add))
                    dve.wait(t)
                    t = dve.mark(V.reciprocal(inverse[:], total[:]))
                    dve.wait(t)
                    for r in range(RT):
                        t = dve.mark(V.tensor_scalar(e2[:, r, :], e2[:, r, :], inverse[:, r:r + 1], None, ALU.mult))
                    dve.wait(t)
                    weighted = dve.mark(V.tensor_reduce(weight[:], e2[:], AX.X, ALU.add))
                    for r in range(RT):
                        i, ps = banks.next()
                        terms = []
                        for k in range(KT):
                            terms += three(x_hi[:, k, r * P:(r + 1) * P], x_lo[:, k, r * P:(r + 1) * P],
                                           we_hi[:, k, :], we_lo[:, k, :])
                        done = products(ps, terms, *banks.free[i])
                        dve.wait(done, weighted)
                        t = dve.mark(V.scalar_tensor_tensor(out=rows[:, r, :], in0=ps, scalar=weight[:, r:r + 1],
                                                            in1=rows[:, r, :], op0=ALU.mult, op1=ALU.add))
                        banks.free[i] = (t,)
                        i, ps = banks.next()
                        terms = []
                        for k in range(KT):
                            terms += three(h_hi[:, k, r * P:(r + 1) * P], h_lo[:, k, r * P:(r + 1) * P],
                                           wd_hi[:, k, :], wd_lo[:, k, :])
                        done = products(ps, terms, hidden, *banks.free[i])
                        dve.wait(done, t)
                        t = dve.mark(V.tensor_tensor(rows[:, r, :], ps, rows[:, r, :], ALU.add))
                        banks.free[i] = (t,)
                    store_rows(1, out, b, rows, t)
                    end_loop()

        kv_projection()
        q_projection_0()
        attention(0)
        out_projection_0()
        ffn_0()
        q_projection_1()
        attention(1)
        out_projection_1()
        ffn_1()


def laid_out(inputs):
    import numpy as np

    f = {k: np.asarray(v) for k, v in inputs.items()}
    c = np.ascontiguousarray
    columns = lambda v: c(v.reshape(KT, P).T)
    row = lambda v: c(v.reshape(-1))
    mask = np.pad(f["mask_BxS2_ik0"], ((0, 0), (0, TT * P - T)))
    return {
        "x": c(f["x"]), "ctx_t": c(f["ctx_2048"].transpose(0, 2, 1)),
        "mask_t": c(mask.reshape(B, TT, P).transpose(2, 0, 1)),
        "wq0": c(f["L0_xattn_wq"]), "bq0": columns(f["L0_xattn_bq"]),
        "wkv0_t": c(f["L0_xattn_wkv"].T),
        "bk0": columns(f["L0_xattn_bkv"][:D]), "bv0": row(f["L0_xattn_bkv"][D:]),
        "wp0": c(f["L0_xattn_wp"]), "bp0": row(f["L0_xattn_bp"]),
        "w1_t": c(f["L0_ffn_W1"].T), "w2_t": c(f["L0_ffn_W2"].T),
        "wq1_t": c(f["L1_xattn_Wq"].T), "bq1": columns(f["L1_xattn_bq"]),
        "wk1_t": c(f["L1_xattn_Wk"].T), "bk1": columns(f["L1_xattn_bk"]),
        "wv1_t": c(f["L1_xattn_Wv"].T), "bv1": row(f["L1_xattn_bv"]),
        "wo1_t": c(f["L1_xattn_Wo"].T), "bo1": row(f["L1_xattn_bo"]),
        "gamma": row(f["L1_xattn_ln_gamma"]), "beta": row(f["L1_xattn_ln_beta"]),
        "rs": c(f["L1_xattn_residual_scale"].reshape(1)),
        "wu_t": c(f["L1_ffn_W_up"].T), "wd_t": c(f["L1_ffn_W_down"].T),
        "wg_t": c(f["L1_ffn_W_gate"].T), "we": c(f["L1_ffn_W_expert"]),
    }


def kernel(**inputs):
    import concourse.bacc as bacc
    from concourse.bass_utils import run_bass_kernel_spmd

    nc = bacc.Bacc("TRN2", target_bir_lowering=False, num_devices=1)
    arrays = {f"in_{k}": v for k, v in laid_out(inputs).items()}
    args = {k[3:]: nc.dram_tensor(k, v.shape, mybir.dt.from_np(v.dtype), kind="ExternalInput").ap()
            for k, v in arrays.items()}
    result = nc.dram_tensor("result", (B, S, D), F32, kind="ExternalOutput").ap()
    build(nc, args, result)
    return run_bass_kernel_spmd(nc, [arrays], core_ids=[0]).results[0]["result"]
```

```python
from contextlib import ExitStack

import concourse.bass as bass
from concourse import mybir

F32 = mybir.dt.float32
F32R = mybir.dt.float32r
BF16 = mybir.dt.bfloat16
I32 = mybir.dt.int32
ALU = mybir.AluOpType
ACT = mybir.ActivationFunctionType
AX = mybir.AxisListType

P = 128
B, S, D, T, H, FF, NE = 4, 512, 512, 1601, 16, 2048, 8
DH = D // H
KT = D // P
RT = S // P
HPG = P // DH
NG = H // HPG
TT = -(-T // P)
TP = T + T % 2
TROWS = [min(P, T - P * i) for i in range(TT)]
KCH = [(0, 402), (402, 400), (802, 400), (1202, 400)]
MCH, MW, MV = [0, 400, 800, 1200], 402, 401
FT = FF // P
MAGIC = 12582912.0
ROOT = float(DH) ** 0.5
POOLED = [0, 1, 3, 5, 7, 9, 11]
FIRST_SUM = 2
LAG = 2
EPS = 1e-5


class Lane:

    def __init__(self, engine, sem):
        self.e, self.sem, self.n, self.seen = engine, sem, 0, {}

    def wait(self, *tokens):
        for t in tokens:
            if t is not None and self.seen.get(id(t[0]), 0) < t[1]:
                self.e.wait_ge(t[0], t[1])
                self.seen[id(t[0])] = t[1]

    def mark(self, instruction):
        instruction.then_inc(self.sem, 1)
        self.n += 1
        return self.sem, self.n


class Core:
    def __init__(self, nc, stack):
        self.nc = nc
        sem = lambda name: stack.enter_context(nc.semaphore(name))
        self.pe = Lane(nc.tensor, sem("pe_done"))
        self.act = Lane(nc.scalar, sem("act_done"))
        self.dve = Lane(nc.vector, sem("dve_done"))
        self.pool = Lane(nc.gpsimd, sem("pool_done"))
        self.sp = Lane(nc.sync, None)
        self.lanes = (self.pe, self.act, self.dve, self.pool, self.sp)
        self.dma_sems = [sem(f"dma_{i}") for i in range(24)]
        self.dma_count = {}

    def dma(self, k, dst, src, *tokens, lane=None):
        lane = lane or self.sp
        lane.wait(*tokens)
        dst, src = (x.bitcast(F32) if x.dtype == F32R else x for x in (dst, src))
        lane.e.dma_start(dst, src).then_inc(self.dma_sems[k], 16)
        self.dma_count[k] = self.dma_count.get(k, 0) + 16
        return self.dma_sems[k], self.dma_count[k]

    def fence(self):
        for k, n in self.dma_count.items():
            self.sp.wait((self.dma_sems[k], n))
        for lane in self.lanes[:4]:
            if lane.n:
                lane.wait((lane.sem, lane.n))
        self.nc.all_engine_barrier()
        for lane in self.lanes[:4]:
            if lane.n:
                lane.e.sem_clear(lane.sem)
        for k in self.dma_count:
            self.sp.e.sem_clear(self.dma_sems[k])
        self.nc.all_engine_barrier()
        for lane in self.lanes:
            lane.n, lane.seen = 0, {}
        self.dma_count = {}


class Ring:

    def __init__(self, buffers):
        self.buffers, self.free, self.at = buffers, [()] * len(buffers), -1

    def next(self):
        self.at = (self.at + 1) % len(self.buffers)
        return self.at, self.buffers[self.at]

    def reset(self):
        self.free, self.at = [()] * len(self.buffers), -1


def at(dram, i):
    if isinstance(i, int):
        return dram[i]
    names = "abcdef"[:len(dram.shape) - 1]
    return dram[bass.ds(i, 1)].rearrange(f"o {' '.join(names)} -> (o {names[0]}) {' '.join(names[1:])}")


def f32(ap):
    return ap.bitcast(F32)


def finish(chain):
    while True:
        try:
            next(chain)
        except StopIteration as end:
            return end.value


def together(*chains):
    values, live = [None] * len(chains), list(range(len(chains)))
    while live:
        for n in list(live):
            try:
                next(chains[n])
            except StopIteration as end:
                values[n] = end.value
                live.remove(n)
    return values


class Side:

    def __init__(self, chain):
        self.chain, self.value = chain, None

    def tick(self, steps=1):
        for _ in range(steps):
            if self.chain is None:
                return
            try:
                next(self.chain)
            except StopIteration as end:
                self.value, self.chain = end.value, None

    def finish(self):
        while self.chain is not None:
            self.tick()
        return self.value


def build(nc, a, out):
    stack = ExitStack()
    with stack:
        core = Core(nc, stack)
        pe, act, dve, pool, sp = core.lanes
        V, A, M, G = nc.vector, nc.scalar, nc.tensor, nc.gpsimd

        psum = stack.enter_context(nc.psum_tensor("psum", [P, 8, 512], F32))
        bank = lambda i: psum[:, i, :]
        banks = Ring([bank(i) for i in range(8)])

        def sbuf(scope, name, shape, dt=F32):
            return scope.enter_context(nc.sbuf_tensor(name, shape, dt))

        ident = sbuf(stack, "ident", [P, P])
        minus_half = sbuf(stack, "minus_half", [P, RT])

        def scratch(name, shape, dt=F32):
            return nc.dram_tensor(name, shape, dt).ap()

        k_hi = [scratch(f"k_hi{n}", (B * NG, P, TP)) for n in range(2)]
        k_lo = [scratch(f"k_lo{n}", (B * NG, P, TP)) for n in range(2)]
        v_rows = [scratch(f"v_rows{n}", (B, TT * P, D)) for n in range(2)]
        q_hi = [scratch(f"q_hi{n}", (B * NG, P, S)) for n in range(2)]
        q_lo = [scratch(f"q_lo{n}", (B * NG, P, S)) for n in range(2)]
        o_t = [scratch(f"o_t{n}", (B * NG, P, S)) for n in range(2)]
        x_mid = [scratch(f"x_mid{n}", (B, S, D)) for n in range(3)]
        x_in = a["x"]

        t0 = pool.mark(G.memset(ident[:], 0.0))
        pool.wait(t0)
        pool.mark(G.affine_select(out=ident[:], in_=ident[:], compare_op=ALU.not_equal, fill=1.0,
                                  base=0, pattern=[[-1, P]], channel_multiplier=1))
        dve.mark(V.memset(minus_half[:], -0.5))
        core.fence()

        def split(hi, lo, src, *tokens):
            act.wait(*tokens)
            h = act.mark(A.activation(hi, src, ACT.Copy))
            dve.wait(h, *tokens)
            return dve.mark(V.tensor_tensor(lo, src, f32(hi), ALU.subtract))

        def load_split_weight(scope, name, dram, stage, width):
            n = dram.shape[0] // P
            hi = sbuf(scope, f"{name}_hi", [P, n, width], F32R)
            lo = sbuf(scope, f"{name}_lo", [P, n, width], F32R)
            done = None
            for k in range(n):
                for c in range(0, width, 512):
                    w = min(512, width - c)
                    i, buf = stage.next()
                    got = core.dma(i, buf[:, 0:w], dram[k * P:(k + 1) * P, c:c + w], *stage.free[i])
                    done = split(hi[:, k, c:c + w], lo[:, k, c:c + w], buf[:, 0:w], got)
                    stage.free[i] = (done,)
                    yield
            return hi, lo, done

        def products(dst, terms, *tokens):
            pe.wait(*tokens)
            for n, (lhs, rhs) in enumerate(terms):
                m = M.matmul(dst, lhs, rhs, start=(n == 0), stop=(n == len(terms) - 1))
            return pe.mark(m)

        def three(l_hi, l_lo, r_hi, r_lo):
            return [(l_hi, r_hi), (l_hi, r_lo), (l_lo, r_hi)]

        def layer_norm(rows, normed, small, *tokens):
            stats, mv, ve, r, t = small
            dve.wait(*tokens)
            for k in range(RT):
                s = dve.mark(V.bn_stats(stats[:, k, :], rows[:, k, :]))
            yield
            dve.wait(s)
            for k in range(RT):
                s = dve.mark(V.bn_aggr(mv[:, k, :], stats[:, k, :]))
            dve.wait(s)
            s = dve.mark(V.tensor_scalar(ve[:], mv[:, :, 1], EPS, None, ALU.add))
            yield
            pool.wait(s)
            s = pool.mark(G.tensor_tensor(r[:], ve[:], minus_half[:], ALU.pow))
            yield
            dve.wait(s)
            s = dve.mark(V.tensor_tensor(t[:], r[:], r[:], ALU.mult))
            dve.wait(s)
            s = dve.mark(V.tensor_tensor(t[:], t[:], ve[:], ALU.mult))
            dve.wait(s)
            s = dve.mark(V.tensor_scalar(t[:], t[:], -0.5, 1.5, ALU.mult, ALU.add))
            dve.wait(s)
            s = dve.mark(V.tensor_tensor(r[:], r[:], t[:], ALU.mult))
            dve.wait(s)
            for k in range(RT):
                s = dve.mark(V.tensor_scalar(normed[:, k, :], rows[:, k, :], mv[:, k, 0:1], r[:, k:k + 1],
                                             ALU.subtract, ALU.mult))
                if k % 2:
                    yield
            return s

        def norm_small(scope, tag):
            return (sbuf(scope, f"stats_{tag}", [P, RT, 6]), sbuf(scope, f"mv_{tag}", [P, RT, 2]),
                    sbuf(scope, f"ve_{tag}", [P, RT]), sbuf(scope, f"r_{tag}", [P, RT]),
                    sbuf(scope, f"t_{tag}", [P, RT]))

        def quantise(rows, scale, recip, *tokens):
            dve.wait(*tokens)
            s = dve.mark(V.tensor_reduce(scale[:], rows[:], AX.X, ALU.max, apply_absolute_value=True))
            yield
            dve.wait(s)
            s = dve.mark(V.tensor_scalar(scale[:], scale[:], 1.0 / 127.0, 1e-8, ALU.mult, ALU.max))
            dve.wait(s)
            s = dve.mark(V.reciprocal(recip[:], scale[:]))
            dve.wait(s)
            for k in range(RT):
                s = dve.mark(V.tensor_scalar(rows[:, k, :], rows[:, k, :], recip[:, k:k + 1], 127.0,
                                             ALU.mult, ALU.min))
            yield
            dve.wait(s)
            s = dve.mark(V.tensor_scalar(rows[:], rows[:], -127.0, MAGIC, ALU.max, ALU.add))
            yield
            dve.wait(s)
            s = dve.mark(V.tensor_scalar(rows[:], rows[:], MAGIC, None, ALU.subtract))
            yield
            return s

        def transposed(rows, use, *tokens, ring=banks):
            for k in range(KT):
                i, dst = ring.next()
                pe.wait(*ring.free[i], *tokens)
                for r in range(RT):
                    m = M.transpose(dst[:, r * P:(r + 1) * P], rows[:, r, k * P:(k + 1) * P], ident[:])
                done = use(k, dst, pe.mark(m))
                ring.free[i] = (done,)
                yield
            return done

        def load_rows(k, dst, dram, i, *tokens):
            return core.dma(k, dst[:], at(dram, i).rearrange("(r p) d -> p r d", p=P), *tokens)

        def store_rows(k, dram, i, src, *tokens):
            return core.dma(k, at(dram, i).rearrange("(r p) d -> p r d", p=P), src[:], *tokens)

        def quantised_weight(scope, name, dram, stage_rows, dma):
            wt = sbuf(scope, f"{name}_t", [P, KT, D], BF16)
            scale = sbuf(scope, f"{name}_scale", [P, KT])
            recip = sbuf(scope, f"{name}_recip", [P, KT])
            got = core.dma(dma, stage_rows[:], dram.rearrange("(r p) d -> p r d", p=P))
            q = yield from quantise(stage_rows, scale, recip, got)

            def keep(k, src, token):
                act.wait(token)
                return act.mark(A.activation(wt[:, k, :], src, ACT.Copy))
            token = yield from transposed(stage_rows, keep, q)
            return wt, scale, token

        def row_of(dst, columns, *tokens):
            i, ps = banks.next()
            pe.wait(*banks.free[i], *tokens)
            for r in range(RT):
                m = M.matmul(ps[:, r * P:(r + 1) * P], columns[:, r:r + 1].to_broadcast([P, P]), ident[:],
                             start=True, stop=True)
            token = pe.mark(m)
            act.wait(token)
            banks.free[i] = (act.mark(A.activation(dst, ps, ACT.Copy)),)
            return banks.free[i][0]

        def start_loop():
            core.fence()
            banks.reset()

        def end_loop():
            core.fence()
            banks.reset()

        def store_q(n, b, g, parts, token, k):
            core.dma(k, at(q_hi[n], b * NG + g), parts[0][:], token)
            return core.dma(k, at(q_lo[n], b * NG + g), parts[1][:], token)

        def kv_and_q_projection():
            with ExitStack() as scope:
                raw = [sbuf(scope, f"ctx_raw{k}", [P, T]) for k in range(KT)]
                stage = Ring([raw[k][:, c:c + 512] for c in (0, 512) for k in range(KT)])
                rows = sbuf(scope, "q0_rows", [P, RT, D])
                small = norm_small(scope, "q0")
                step = sbuf(scope, "q0_step", [P, RT])
                recip = sbuf(scope, "q0_recip", [P, RT])
                step_row = sbuf(scope, "q0_step_row", [P, S])
                xq_t = sbuf(scope, "q0_xq_t", [P, KT, S], BF16)
                bq = sbuf(scope, "q0_bq", [P, KT])
                full = sbuf(scope, "q0_full", [P, S])
                parts = [sbuf(scope, f"q0_part{j}", [P, S], F32R) for j in range(2)]
                QUANTISED = 8
                wq = Side(quantised_weight(scope, "wq0", a["wq0"], rows, QUANTISED))
                core.dma(QUANTISED + 1, bq[:], a["bq0"])
                wk, wv, bk, bv = [], [], [], []
                for n, (kd, vd) in enumerate(((a["wkv0_t"][:, 0:D], a["wkv0_t"][:, D:2 * D]),
                                              (a["wk1_t"], a["wv1_t"]))):
                    for kept, name, dram in ((wk, f"wk{n}", kd), (wv, f"wv{n}", vd)):
                        weight = Side(load_split_weight(scope, name, dram, stage, D))
                        while weight.chain is not None:
                            weight.tick()
                            wq.tick()
                        kept.append(weight.value)
                    bk.append(sbuf(scope, f"bk{n}", [P, KT]))
                    bv.append(sbuf(scope, f"bv{n}", [P, D]))
                    core.dma(QUANTISED + 2, bk[n][:], a[f"bk{n}"])
                    core.dma(QUANTISED + 2, bv[n][:], a[f"bv{n}"].partition_broadcast(P))
                wt, w_step, _ = wq.finish()
                c_hi = sbuf(scope, "ctx_hi", [P, KT, TP], F32R)
                c_lo = sbuf(scope, "ctx_lo", [P, KT, TP], F32R)
                kt_hi = [sbuf(scope, f"kt_hi{i}", [P, TP], F32R) for i in range(2)]
                kt_lo = [sbuf(scope, f"kt_lo{i}", [P, TP], F32R) for i in range(2)]
                v_out = [sbuf(scope, f"v_out{i}", [P, D]) for i in range(4)]
                dve.mark(V.memset(f32(c_hi[:, :, T:TP]), 0.0))
                dve.mark(V.memset(f32(c_lo[:, :, T:TP]), 0.0))

                def q_of(b):
                    got = load_rows(QUANTISED, rows, x_in, b)
                    yield
                    s = yield from layer_norm(rows, rows, small, got)
                    s = yield from quantise(rows, step, recip, s)
                    stepped = row_of(step_row[:], step, s)
                    yield

                    def keep(k, src, token):
                        act.wait(token)
                        return act.mark(A.activation(xq_t[:, k, :], src, ACT.Copy))
                    ready = yield from transposed(rows, keep, s)
                    yield
                    free = ()
                    for g in range(NG):
                        i, ps = banks.next()
                        done = products(ps, [(wt[:, k, g * P:(g + 1) * P], xq_t[:, k, :]) for k in range(KT)],
                                        ready, *banks.free[i])
                        dve.wait(done, stepped, *free)
                        t = dve.mark(V.scalar_tensor_tensor(out=full[:], in0=ps, scalar=w_step[:, g:g + 1],
                                                            in1=step_row[:], op0=ALU.mult, op1=ALU.mult))
                        banks.free[i] = (t,)
                        dve.wait(t)
                        h = dve.mark(V.tensor_scalar(parts[0][:], full[:], bq[:, g:g + 1], None, ALU.add))
                        dve.wait(h)
                        l = dve.mark(V.scalar_tensor_tensor(out=parts[1][:], in0=full[:], scalar=bq[:, g:g + 1],
                                                            in1=f32(parts[0][:]), op0=ALU.add, op1=ALU.subtract))
                        free = (store_q(0, b, g, parts, l, QUANTISED + 1), l)
                        yield
                        yield

                def load_context(b, *tokens):
                    src = at(a["ctx_t"], b)
                    for k in range(KT):
                        core.dma(k, raw[k][:], src[k * P:(k + 1) * P, :], *tokens)

                def k_terms(n, g, k, c0, cw):
                    w_hi, w_lo, _ = wk[n]
                    return three(w_hi[:, k, g * P:(g + 1) * P], w_lo[:, k, g * P:(g + 1) * P],
                                 c_hi[:, k, c0:c0 + cw], c_lo[:, k, c0:c0 + cw])

                def batch(b, more):
                    side = Side(q_of(b))
                    ready = [split(c_hi[:, k, 0:T], c_lo[:, k, 0:T], raw[k][:]) for k in range(KT)]
                    if more:
                        load_context(b + 1, *ready)
                    opened = []
                    for c0, cw in KCH:
                        opened.append(banks.next())
                    for k in range(KT):
                        pe.wait(ready[k])
                        for (i, ps), (c0, cw) in zip(opened, KCH):
                            for m_, (lhs, rhs) in enumerate(k_terms(0, 0, k, c0, cw)):
                                m = M.matmul(ps[:, 0:cw], lhs, rhs, start=(k == 0 and m_ == 0),
                                             stop=(k == KT - 1 and m_ == 2))
                            done = pe.mark(m)
                    first_done = done
                    kt_free = [(), ()]
                    v_free = [()] * 4
                    nk = nv = 0
                    for n in range(2):
                        for g in range(NG):
                            s = nk % 2
                            nk += 1
                            for c, (c0, cw) in enumerate(KCH):
                                if n == g == 0:
                                    (i, ps), done = opened[c], first_done
                                else:
                                    i, ps = banks.next()
                                    terms = []
                                    for k in range(KT):
                                        terms += k_terms(n, g, k, c0, cw)
                                    done = products(ps[:, 0:cw], terms, *banks.free[i])
                                act.wait(done, *kt_free[s])
                                h = act.mark(A.activation(kt_hi[s][:, c0:c0 + cw], ps[:, 0:cw], ACT.Identity,
                                                          bias=bk[n][:, g:g + 1]))
                                dve.wait(h, *kt_free[s])
                                banks.free[i] = (dve.mark(V.scalar_tensor_tensor(
                                    out=kt_lo[s][:, c0:c0 + cw], in0=ps[:, 0:cw], scalar=bk[n][:, g:g + 1],
                                    in1=f32(kt_hi[s][:, c0:c0 + cw]), op0=ALU.add, op1=ALU.subtract)),)
                                if not n == g == 0:
                                    side.tick()
                            core.dma(4 + s, at(k_hi[n], b * NG + g), kt_hi[s][:], h)
                            kt_free[s] = (core.dma(4 + s, at(k_lo[n], b * NG + g), kt_lo[s][:],
                                                   *banks.free[i]),)
                        w_hi, w_lo, _ = wv[n]
                        for t, height in enumerate(TROWS):
                            s = nv % 4
                            nv += 1
                            i, ps = banks.next()
                            terms = []
                            for k in range(KT):
                                terms += three(c_hi[:, k, t * P:t * P + height], c_lo[:, k, t * P:t * P + height],
                                               w_hi[:, k, :], w_lo[:, k, :])
                            done = products(ps[0:height, :], terms, *banks.free[i])
                            dve.wait(done, *v_free[s])
                            banks.free[i] = (dve.mark(V.tensor_tensor(v_out[s][0:height, :], ps[0:height, :],
                                                                      bv[n][0:height, :], ALU.add)),)
                            v_free[s] = (core.dma(12 + s, at(v_rows[n], b)[t * P:t * P + height, :],
                                                  v_out[s][0:height, :], *banks.free[i]),)
                            side.tick()
                    side.finish()
                    end_loop()

                load_context(0, (dve.sem, dve.n), (act.sem, act.n))
                start_loop()
                with nc.Fori(0, B - 1) as b:
                    batch(b, True)
                batch(B - 1, False)

        def q_projection_1():
            with ExitStack() as scope:
                bq = sbuf(scope, "q1_bq", [P, KT])
                stage = Ring([sbuf(scope, f"q1_stage{i}", [P, 512]) for i in range(4)])
                w_hi, w_lo, _ = finish(load_split_weight(scope, "wq1", a["wq1_t"], stage, D))
                core.dma(5, bq[:], a["bq1"])

                def slot(n):
                    return (sbuf(scope, f"q1_rows{n}", [P, RT, D]), norm_small(scope, f"q1_{n}"),
                            sbuf(scope, f"q1_x_hi{n}", [P, KT, S], F32R), sbuf(scope, f"q1_x_lo{n}", [P, KT, S], F32R),
                            [[sbuf(scope, f"q1_part{n}{i}{j}", [P, S], F32R) for j in range(2)] for i in range(2)])

                def q_of(b, buffers, dma):
                    rows, small, x_hi, x_lo, parts = buffers
                    got = load_rows(dma, rows, x_mid[1], b)
                    yield
                    s = yield from layer_norm(rows, rows, small, got)
                    ready = yield from transposed(
                        rows, lambda k, src, t: split(x_hi[:, k, :], x_lo[:, k, :], src, t), s)
                    free = [(), ()]
                    for g in range(NG):
                        i, ps = banks.next()
                        terms = []
                        for k in range(KT):
                            terms += three(w_hi[:, k, g * P:(g + 1) * P], w_lo[:, k, g * P:(g + 1) * P],
                                           x_hi[:, k, :], x_lo[:, k, :])
                        done = products(ps, terms, ready, *banks.free[i])
                        hi, lo = parts[g % 2]
                        act.wait(done, *free[g % 2])
                        h = act.mark(A.activation(hi[:], ps, ACT.Identity, bias=bq[:, g:g + 1]))
                        dve.wait(h, *free[g % 2])
                        l = dve.mark(V.scalar_tensor_tensor(out=lo[:], in0=ps, scalar=bq[:, g:g + 1],
                                                            in1=f32(hi[:]), op0=ALU.add, op1=ALU.subtract))
                        banks.free[i] = (l,)
                        free[g % 2] = (store_q(1, b, g, (hi, lo), l, dma + 1 + g % 2),)
                        yield

                slots = [slot(n) for n in range(2)]
                start_loop()
                with nc.Fori(0, B // 2) as pair:
                    together(*[q_of(pair * 2 + n, slots[n], 8 * n) for n in range(2)])
                    end_loop()

        def attention(n):
            first = n == 0
            NQ = 3 if first else 4
            with ExitStack() as scope:
                k_st = [sbuf(scope, f"k_st{n}{s}", [P, HPG, TP], F32R) for s in range(NG)]
                q_st = [sbuf(scope, f"q_st{n}{s}", [P, HPG, S], F32R) for s in range(NG)]
                v_st = [sbuf(scope, f"v_st{n}{s}", [P, TT, P]) for s in range(2)]
                probs = Ring([sbuf(scope, f"probs{n}{i}", [P, HPG, S]) for i in range(4)])
                pooled = sbuf(scope, f"pooled{n}", [P, HPG, S])
                ones = sbuf(scope, f"ones{n}", [P, DH])
                acc_sb = sbuf(scope, f"acc_sb{n}", [P, S])
                den_sb = sbuf(scope, f"den_sb{n}", [P, S])
                rec = sbuf(scope, f"rec{n}", [P, S])
                o_sb = sbuf(scope, f"o_sb{n}", [P, S])
                W = 1 if first else 2
                if first:
                    scores = Ring([psum[:, i:i + 1, :] for i in range(2)])
                    windows = Ring([psum[:, 2:4, :], psum[:, 4:6, :]])
                else:
                    scores = Ring([psum[:, 2 * i:2 * i + 2, :] for i in range(3)])
                    windows = Ring([])
                acc, den = bank(6), bank(7)
                dve.mark(V.memset(ones[:], 1.0))
                if first:
                    neg_max = sbuf(scope, "neg_max", [P, HPG, RT, DH])
                    win_max = sbuf(scope, "win_max", [P, HPG, RT, 2])
                    max_hi = sbuf(scope, "max_hi", [P, HPG, RT], F32R)
                    dve.mark(V.memset(neg_max[:], 0.0))
                    dve.mark(V.memset(f32(k_st[0][96:128, :, :]), 1.0))
                    for s in range(1, NG):
                        pool.mark(G.memset(f32(k_st[s][96:128, :, :]), 1.0))
                else:
                    mask_i = sbuf(scope, "mask_i", [P, B, TT], I32)
                    bound = sbuf(scope, "bound", [P, B, TT])
                    top = sbuf(scope, "top", [P, TT])
                    got = core.dma(9, mask_i[:], a["mask_t"])
                    dve.wait(got)
                    s_ = dve.mark(V.tensor_scalar(bound[:], mask_i[:], 0.5, 100.0 * ROOT, ALU.is_gt, ALU.mult))
                    dve.wait(s_)
                    dve.mark(V.tensor_scalar(bound[:], bound[:], 50.0 * ROOT, None, ALU.subtract))

                loaded = {}

                def load(s, unit, *tokens):
                    for quarter in range(NQ):
                        rows = slice(quarter * DH, (quarter + 1) * DH)
                        k_src = (k_hi, k_lo, k_hi, k_lo)[quarter][n]
                        q_src = (q_hi, q_hi, q_lo, q_lo)[quarter][n]
                        core.dma(s, k_st[s][rows, :, :], at(k_src, unit).rearrange("(j d) t -> d j t", d=DH),
                                 *tokens)
                        loaded[s] = core.dma(s, q_st[s][rows, :, :],
                                             at(q_src, unit).rearrange("(j d) t -> d j t", d=DH))

                def load_v(b, g, *tokens):
                    s = g % 2
                    v_src = at(v_rows[n], b)[:, g * P:(g + 1) * P]
                    core.dma(4 + s, v_st[s][:, 0:TT - 1, :],
                             v_src[0:(TT - 1) * P, :].rearrange("(t p) c -> p t c", p=P), *tokens)
                    loaded[4 + s] = core.dma(4 + s, v_st[s][0:TROWS[-1], TT - 1, :], v_src[(TT - 1) * P:T, :])

                def max_pass(s):
                    pieces, done = [], {}

                    def window(j, r, c):
                        i, ps = windows.next()
                        pe.wait(loaded.get(s), *windows.free[i])
                        for w in range(2):
                            start = MCH[2 * c + w]
                            m = M.matmul(ps[:, w, 0:MW], q_st[s][0:96, j, r * P:(r + 1) * P],
                                         k_st[s][0:96, j, start:start + MW], start=True, stop=True)
                        m = pe.mark(m)
                        dve.wait(m)
                        done[j] = dve.mark(V.tensor_reduce(win_max[:, j, r, c:c + 1], ps[:, :, 0:MV], AX.XY, ALU.max))
                        windows.free[i] = (done[j],)

                    def columns(j):
                        two = slice(j, j + 2)
                        dve.wait(done[j + 1])
                        t = dve.mark(V.tensor_reduce(neg_max[:, two, :, 0], win_max[:, two, :, :], AX.X, ALU.max,
                                                     negate=True))
                        dve.wait(t)
                        t = dve.mark(V.tensor_copy(max_hi[:, two, :], neg_max[:, two, :, 0]))
                        dve.wait(t)
                        done[j] = dve.mark(V.tensor_tensor(neg_max[:, two, :, 1], neg_max[:, two, :, 0],
                                                           f32(max_hi[:, two, :]), ALU.subtract))

                    def turn(j):
                        i, ps = windows.next()
                        pe.wait(done[j], *windows.free[i])
                        for jj in range(2):
                            for r in range(RT):
                                m = M.matmul(ps[96:128, jj, r * P:(r + 1) * P], neg_max[:, j + jj, r, :], ident[:],
                                             start=True, stop=True)
                        t = pe.mark(m)
                        dve.wait(t)
                        max_ready[s] = dve.mark(V.tensor_copy(q_st[s][96:128, j:j + 2, :], ps[96:128, :, :]))
                        windows.free[i] = (max_ready[s],)

                    for j in range(HPG):
                        for r in range(RT):
                            for c in range(2):
                                pieces.append(lambda j=j, r=r, c=c: window(j, r, c))
                                if j == 2 and r == 1 and c == 0:
                                    pieces.append(lambda: turn(0))
                        if j % 2:
                            pieces.append(lambda j=j: columns(j - 1))
                    pieces.append(lambda: None)
                    pieces.append(lambda: turn(2))
                    return pieces

                max_ready = {}
                state = {}

                tiles = {}

                def begin(g, t):
                    pi, pr = probs.next()
                    tiles[g, t] = (pi, pr, [], probs.free[pi])
                    probs.free[pi] = ()

                def score(g, t, j):
                    rows = TROWS[t]
                    pi, pr, done, buffer_free = tiles[g, t]
                    i, ps = scores.next()
                    pe.wait(loaded.get(g), max_ready.get(g), *scores.free[i])
                    for w in range(W):
                        m = M.matmul(ps[0:rows, w, :], k_st[g][:, j + w, t * P:t * P + rows],
                                     q_st[g][:, j + w, :], start=True, stop=True)
                    m = state["scored"] = pe.mark(m)
                    dst = pr[0:rows, j:j + W, :]
                    if first:
                        act.wait(m, *buffer_free)
                        e = act.mark(A.activation(dst, ps[0:rows], ACT.Exp, scale=1.0 / ROOT))
                        scores.free[i] = (e,)
                    else:
                        dve.wait(m, *buffer_free)
                        c = dve.mark(V.tensor_scalar(dst, ps[0:rows], top[0:rows, t:t + 1], -50.0 * ROOT,
                                                     ALU.min, ALU.max))
                        scores.free[i] = (c,)
                        act.wait(c)
                        e = act.mark(A.activation(dst, dst, ACT.Exp, scale=1.0 / ROOT))
                    done.append(e)

                def pool_sum(g, t):
                    k = POOLED.index(t) if t in POOLED else 0
                    if not k:
                        return
                    before = tiles[g, POOLED[0]] if k == 1 else None
                    pool.wait(*tiles[g, t][2], state.get("pool"), *(state.get("pooled_free", ()) if k == 1 else ()))
                    state["pool"] = pool.mark(G.tensor_tensor(pooled[:], before[1][:] if before else pooled[:],
                                                              tiles[g, t][1][:], ALU.add))
                    probs.free[tiles[g, t][0]] += (state["pool"],)
                    if before:
                        probs.free[before[0]] += (state["pool"],)

                def values(g, t):
                    rows = TROWS[t]
                    pi, pr, done, _ = tiles[g, t]
                    pe.wait(*done, loaded.get(4 + g % 2))
                    if t == 0:
                        pe.wait(*state.get("acc_free", ()))
                    for j in range(HPG):
                        m = M.matmul(acc[j * DH:(j + 1) * DH, :], v_st[g % 2][0:rows, t, j * DH:(j + 1) * DH],
                                     pr[0:rows, j, :], start=(t == 0), stop=(t == TT - 1))
                    probs.free[pi] += (pe.mark(m),)

                def sums(g, t):
                    if t not in POOLED:
                        rows = TROWS[t]
                        pi, pr, done, _ = tiles[g, t]
                        for j in range(HPG):
                            m = M.matmul(den[j * DH:(j + 1) * DH, :], ones[0:rows, :], pr[0:rows, j, :],
                                         start=(t == FIRST_SUM), stop=False)
                        probs.free[pi] += (pe.mark(m),)
                    if t == TT - 1:
                        pe.wait(state["pool"])
                        for j in range(HPG):
                            m = M.matmul(den[j * DH:(j + 1) * DH, :], ones[:], pooled[:, j, :],
                                         start=False, stop=True)
                        state["summed"] = pe.mark(m)
                        state["pooled_free"] = (state["summed"],)

                def normalise(unit):
                    def copy_out():
                        act.wait(state["summed"], *state.get("sb_free", ()))
                        d = act.mark(A.activation(den_sb[:], den, ACT.Copy))
                        c = act.mark(A.activation(acc_sb[:], acc, ACT.Copy))
                        state["acc_free"] = (c,)
                        state["copied"] = (d, c)

                    def invert(quarter):
                        at_ = slice(quarter * P, (quarter + 1) * P)
                        dve.wait(*state["copied"], *state.get("sb_free", ()))
                        state["inverse"] = dve.mark(V.reciprocal(rec[:, at_], den_sb[:, at_]))

                    def again():
                        dve.wait(state["inverse"])
                        u = dve.mark(V.scalar_tensor_tensor(out=den_sb[:], in0=den_sb[:], scalar=-1.0, in1=rec[:],
                                                            op0=ALU.mult, op1=ALU.mult))
                        dve.wait(u)
                        state["inverse"] = dve.mark(V.scalar_tensor_tensor(
                            out=rec[:], in0=den_sb[:], scalar=2.0 - 1e-8, in1=rec[:], op0=ALU.add, op1=ALU.mult))

                    def scaled():
                        dve.wait(state["inverse"], *state.get("o_free", ()))
                        o = dve.mark(V.tensor_tensor(o_sb[:], acc_sb[:], rec[:], ALU.mult))
                        state["sb_free"] = (o,)
                        state["o_free"] = (core.dma(8, at(o_t[n], unit), o_sb[:], o),)

                    pieces = [copy_out] + [lambda q=q: invert(q) for q in range(S // P)]
                    return pieces + ([] if first else [again]) + [scaled]

                def run_all(pieces):
                    for piece in pieces:
                        piece()

                def batch(b, more):
                    if not first:
                        top_ready = dve.mark(V.tensor_copy(top[:], bound[:, b, :] if isinstance(b, int) else
                                                           bound[:, bass.ds(b, 1), :].rearrange("p o t -> p (o t)")))
                        dve.wait(top_ready)
                    tiles.clear()
                    todo, total, ran, scored = [], [0], [0], {}

                    def tick():
                        ran[0] += 1
                        while todo and (total[0] - len(todo)) * (4 * TT - 2) < total[0] * ran[0]:
                            todo.pop(0)()

                    for step in range(NG * TT + LAG):
                        g, t = divmod(step, TT)
                        vg, vt = divmod(step - LAG, TT)
                        if g < NG and t == 0:
                            run_all(todo)
                            todo[:] = max_pass((g + 1) % NG) if first and (g + 1 < NG or more) else []
                            total[0], ran[0] = len(todo), 0
                            ahead = g + 2
                            if ahead < NG or more:
                                nb = b if ahead < NG else b + 1
                                load(ahead % NG, nb * NG + ahead % NG, scored.get(ahead - NG))
                        if g < NG:
                            begin(g, t)
                            for j in range(0, HPG // 2, W):
                                score(g, t, j)
                            tick()
                        if step >= LAG:
                            values(vg, vt)
                            tick()
                        if g < NG:
                            for j in range(HPG // 2, HPG, W):
                                score(g, t, j)
                            if t == TT - 1:
                                scored[g] = state["scored"]
                            tick()
                        if step >= LAG:
                            if vt == FIRST_SUM:
                                pe.wait(*state.get("acc_free", ()))
                            sums(vg, vt)
                            if vt == TT - 1:
                                if vg + 2 < NG or more:
                                    load_v(b if vg + 2 < NG else b + 1, (vg + 2) % NG, state["summed"])
                                new = normalise(b * NG + vg)
                                new.pop(0)()
                                todo[:] = new + todo
                                total[0] += len(new)
                        if g < NG:
                            pool_sum(g, t)
                        tick()
                    run_all(todo)

                def reset():
                    core.fence()
                    for ring in (probs, scores, windows):
                        ring.reset()
                    loaded.clear()
                    max_ready.clear()
                    state.clear()

                load(0, 0)
                load_v(0, 0)
                load(1, 1)
                load_v(0, 1)
                if first:
                    pe.wait((dve.sem, dve.n))
                    run_all(max_pass(0))
                reset()
                with nc.Fori(0, B - 1) as b:
                    batch(b, True)
                    reset()
                batch(B - 1, False)
                reset()
                banks.reset()

        def out_projection_and_ffn_0():
            with ExitStack() as scope:
                rows = sbuf(scope, "f0_rows", [P, RT, D])
                cols = sbuf(scope, "f0_cols", [P, RT, D])
                o_rows = sbuf(scope, "o0_rows", [P, RT, D])
                step = sbuf(scope, "o0_step", [P, RT])
                recip = sbuf(scope, "o0_recip", [P, RT])
                oq_t = sbuf(scope, "o0_oq_t", [P, KT, S], BF16)
                w_row = sbuf(scope, "o0_w_row", [P, D])
                bp = sbuf(scope, "o0_bp", [P, D])
                y = [sbuf(scope, f"o0_y{i}", [P, D]) for i in range(2)]
                residual = sbuf(scope, "f0_residual", [P, RT, D])
                code = [sbuf(scope, f"f0_code{i}", [P, S]) for i in range(2)]
                small = norm_small(scope, "f0")
                x_hi = sbuf(scope, "f0_x_hi", [P, KT, S], F32R)
                x_lo = sbuf(scope, "f0_x_lo", [P, KT, S], F32R)
                g_hi = [sbuf(scope, f"f0_g_hi{i}", [P, S], F32R) for i in range(2)]
                g_lo = [sbuf(scope, f"f0_g_lo{i}", [P, S], F32R) for i in range(2)]
                hidden = Ring([bank(i) for i in range(4)])
                PROJECTION = 8

                def projected(b, *tokens):
                    for g in range(NG):
                        got = core.dma(PROJECTION, cols[:, g, :], at(o_t[0], b * NG + g), *tokens)
                    got_x = load_rows(PROJECTION + 1, rows, x_in, b, *tokens)
                    yield

                    def keep_rows(k, src, token):
                        act.wait(token)
                        return act.mark(A.activation(o_rows[:, k, :], src, ACT.Copy))
                    s = yield from transposed(cols, keep_rows, got, ring=hidden)
                    s = yield from quantise(o_rows, step, recip, s)

                    def keep(k, src, token):
                        act.wait(token)
                        return act.mark(A.activation(oq_t[:, k, :], src, ACT.Copy))
                    ready = yield from transposed(o_rows, keep, s, ring=hidden)
                    yield
                    free = [(), ()]
                    for r in range(RT):
                        i, ps = hidden.next()
                        done = products(ps, [(oq_t[:, k, r * P:(r + 1) * P], wt[:, k, :]) for k in range(KT)],
                                        ready, *hidden.free[i])
                        dve.wait(done, *free[r % 2])
                        t = dve.mark(V.scalar_tensor_tensor(out=y[r % 2][:], in0=ps, scalar=step[:, r:r + 1],
                                                            in1=w_row[:], op0=ALU.mult, op1=ALU.mult))
                        hidden.free[i] = (t,)
                        dve.wait(t, got_x)
                        t = dve.mark(V.tensor_tensor(y[r % 2][:], y[r % 2][:], bp[:], ALU.add))
                        dve.wait(t)
                        t = dve.mark(V.tensor_tensor(rows[:, r, :], rows[:, r, :], y[r % 2][:], ALU.add))
                        free[r % 2] = (t,)
                        yield
                    return (yield from layer_norm(rows, cols, small, t))

                def operand(s, *tokens):
                    return transposed(cols, lambda k, src, t: split(x_hi[:, k, :], x_lo[:, k, :], src, t, *tokens),
                                      s, ring=hidden)

                def batch(b, more):
                    side = Side(iter(()))
                    for r in range(RT):
                        copied = act.mark(A.activation(residual[:, r, :], rows[:, r, :], ACT.Copy))
                    if more:
                        side = Side(projected(b + 1, copied))
                    freed, made, last = {}, {}, {}

                    def first_half(f):
                        i, ps = hidden.next()
                        terms = []
                        for k in range(KT):
                            terms += three(w1_hi[:, k, f * P:(f + 1) * P], w1_lo[:, k, f * P:(f + 1) * P],
                                           x_hi[:, k, :], x_lo[:, k, :])
                        done = products(ps, terms, *hidden.free[i])
                        last["x"] = done
                        q = code[f % 2]
                        dve.wait(done, *freed.get(f - 2, ()))
                        t = dve.mark(V.tensor_scalar(q[:], ps, 10.0, -32768.0, ALU.mult, ALU.max))
                        hidden.free[i] = (t,)
                        dve.wait(t)
                        t = dve.mark(V.tensor_scalar(q[:], q[:], 32767.0, MAGIC, ALU.min, ALU.add))
                        dve.wait(t)
                        t = dve.mark(V.tensor_scalar(q[:], q[:], MAGIC, 0.1, ALU.subtract, ALU.mult))
                        act.wait(t, *freed.get(f - 2, ()))
                        t = act.mark(A.activation(q[:], q[:], ACT.Gelu_apprx_tanh))
                        act.wait(t)
                        made[f] = split(g_hi[f % 2][:], g_lo[f % 2][:], q[:], t, *freed.get(f - 2, ()))

                    def second_half(f):
                        pe.wait(made[f])
                        for r in range(RT):
                            terms = three(g_hi[f % 2][:, r * P:(r + 1) * P], g_lo[f % 2][:, r * P:(r + 1) * P],
                                          w2_hi[:, f, :], w2_lo[:, f, :])
                            for m_, (lhs, rhs) in enumerate(terms):
                                m = M.matmul(bank(4 + r), lhs, rhs, start=(f == 0 and m_ == 0),
                                             stop=(f == FT - 1 and m_ == 2))
                        freed[f] = (pe.mark(m),)

                    first_half(0)
                    for f in range(FT):
                        if f + 1 < FT:
                            first_half(f + 1)
                            side.tick()
                        elif more:
                            finish(operand(side.finish(), last["x"]))
                        second_half(f)
                        side.tick()
                    dve.wait(*freed[FT - 1])
                    for r in range(RT):
                        t = dve.mark(V.tensor_tensor(residual[:, r, :], bank(4 + r), residual[:, r, :], ALU.add))
                    store_rows(0, x_mid[1], b, residual, t)
                    core.fence()
                    hidden.reset()

                core.dma(PROJECTION + 2, bp[:], a["bp0"].partition_broadcast(P))
                wt, w_step, _ = finish(quantised_weight(scope, "wp0", a["wp0"], o_rows, PROJECTION))
                row_of(w_row[:], w_step, (dve.sem, dve.n))
                core.fence()
                banks.reset()
                first = Side(projected(0))
                stage = Ring([residual[:, r, :] for r in range(RT)] + [code[0][:], code[1][:]])
                weights = []
                for name, dram, width in (("w1", a["w1_t"], FF), ("w2", a["w2_t"], D)):
                    weight = Side(load_split_weight(scope, name, dram, stage, width))
                    while weight.chain is not None:
                        weight.tick()
                        first.tick()
                    weights.append(weight.value)
                (w1_hi, w1_lo, _), (w2_hi, w2_lo, _) = weights
                finish(operand(first.finish()))
                core.fence()
                hidden.reset()
                with nc.Fori(0, B - 1) as b:
                    batch(b, True)
                batch(B - 1, False)

        def out_projection_and_ffn_1():
            with ExitStack() as scope:
                o_cols = sbuf(scope, "o1_cols", [P, KT, S])
                o_hi = sbuf(scope, "o1_hi", [P, KT, S], F32R)
                o_lo = sbuf(scope, "o1_lo", [P, KT, S], F32R)
                rows = sbuf(scope, "f1_rows", [P, RT, D])
                delta = sbuf(scope, "o1_delta", [P, RT, D])
                bo = sbuf(scope, "o1_bo", [P, D])
                gamma = sbuf(scope, "o1_gamma", [P, D])
                beta = sbuf(scope, "o1_beta", [P, D])
                rs = sbuf(scope, "o1_rs", [P, 1])
                residual = sbuf(scope, "f1_residual", [P, RT, D])
                small = norm_small(scope, "f1")
                x_hi = sbuf(scope, "f1_x_hi", [P, KT, S], F32R)
                x_lo = sbuf(scope, "f1_x_lo", [P, KT, S], F32R)
                h_hi = sbuf(scope, "f1_h_hi", [P, KT, S], F32R)
                h_lo = sbuf(scope, "f1_h_lo", [P, KT, S], F32R)
                logits = sbuf(scope, "f1_logits", [P, RT, NE])
                top = sbuf(scope, "f1_top", [P, RT, NE])
                e2 = sbuf(scope, "f1_e2", [P, RT, 2])
                total = sbuf(scope, "f1_total", [P, RT])
                inverse = sbuf(scope, "f1_inverse", [P, RT])
                weight = sbuf(scope, "f1_weight", [P, RT])
                PROJECTION = 8

                def projected(b, *tokens):
                    got = [core.dma(PROJECTION + g, o_cols[:, g, :], at(o_t[1], b * NG + g), *tokens)
                           for g in range(NG)]
                    got_x = load_rows(PROJECTION + NG, rows, x_mid[1], b, *tokens)
                    yield
                    for g in range(NG):
                        ready = split(o_hi[:, g, :], o_lo[:, g, :], o_cols[:, g, :], got[g])
                        if g % 2:
                            yield
                    for r in range(RT):
                        i, ps = banks.next()
                        terms = []
                        for k in range(KT):
                            terms += three(o_hi[:, k, r * P:(r + 1) * P], o_lo[:, k, r * P:(r + 1) * P],
                                           w_hi[:, k, :], w_lo[:, k, :])
                        done = products(ps, terms, ready, *banks.free[i])
                        dve.wait(done)
                        t = dve.mark(V.tensor_tensor(delta[:, r, :], ps, bo[:], ALU.add))
                        banks.free[i] = (t,)
                        dve.wait(t)
                        t = dve.mark(V.tensor_scalar(delta[:, r, :], delta[:, r, :], rs[:, 0:1], None, ALU.mult))
                        pool.wait(got_x)
                        u = pool.mark(G.tensor_tensor(rows[:, r, :], rows[:, r, :], beta[:], ALU.add))
                        yield
                    s = yield from layer_norm(delta, delta, small, t)
                    dve.wait(s, u)
                    for r in range(RT):
                        t = dve.mark(V.tensor_tensor(delta[:, r, :], delta[:, r, :], gamma[:], ALU.mult))
                        dve.wait(t)
                        t = dve.mark(V.tensor_tensor(rows[:, r, :], rows[:, r, :], delta[:, r, :], ALU.add))
                        yield
                    return (yield from layer_norm(rows, delta, small, t))

                def operand(s, *tokens):
                    return transposed(delta, lambda k, src, t: split(x_hi[:, k, :], x_lo[:, k, :], src, t, *tokens), s)

                def batch(b, more):
                    side = Side(iter(()))
                    for r in range(RT):
                        copied = act.mark(A.activation(residual[:, r, :], rows[:, r, :], ACT.Copy))
                    if more:
                        side = Side(projected(b + 1, copied))
                    for r in range(RT):
                        i, ps = banks.next()
                        terms = []
                        for k in range(KT):
                            terms += three(x_hi[:, k, r * P:(r + 1) * P], x_lo[:, k, r * P:(r + 1) * P],
                                           wg_hi[:, k, :], wg_lo[:, k, :])
                        done = products(ps[:, 0:NE], terms, *banks.free[i])
                        dve.wait(done)
                        t = dve.mark(V.tensor_copy(logits[:, r, :], ps[:, 0:NE]))
                        banks.free[i] = (t,)
                        dve.wait(t)
                        t = dve.mark(V.max(top[:, r, :], logits[:, r, :]))
                    side.tick()
                    dve.wait(t)
                    for r in range(RT):
                        t = dve.mark(V.tensor_scalar(e2[:, r, :], top[:, r, 0:2], top[:, r, 0:1], None, ALU.subtract))
                    act.wait(t)
                    t = act.mark(A.activation(e2[:], e2[:], ACT.Exp))
                    dve.wait(t)
                    t = dve.mark(V.tensor_reduce(total[:], e2[:], AX.X, ALU.add))
                    dve.wait(t)
                    t = dve.mark(V.reciprocal(inverse[:], total[:]))
                    dve.wait(t)
                    for r in range(RT):
                        t = dve.mark(V.tensor_scalar(e2[:, r, :], e2[:, r, :], inverse[:, r:r + 1], None, ALU.mult))
                    dve.wait(t)
                    weighted = dve.mark(V.tensor_reduce(weight[:], e2[:], AX.X, ALU.add))
                    side.tick()
                    for f in range(KT):
                        i, ps = banks.next()
                        terms = []
                        for k in range(KT):
                            terms += three(wu_hi[:, k, f * P:(f + 1) * P], wu_lo[:, k, f * P:(f + 1) * P],
                                           x_hi[:, k, :], x_lo[:, k, :])
                        done = products(ps, terms, *banks.free[i])
                        act.wait(done)
                        h = act.mark(A.activation(h_hi[:, f, :], ps, ACT.Relu))
                        dve.wait(h)
                        hidden = dve.mark(V.scalar_tensor_tensor(out=h_lo[:, f, :], in0=ps, scalar=0.0,
                                                                 in1=f32(h_hi[:, f, :]), op0=ALU.max,
                                                                 op1=ALU.subtract))
                        banks.free[i] = (hidden,)
                        side.tick(2)
                    dve.wait(copied)
                    for r in range(RT):
                        i, ps = banks.next()
                        terms = []
                        for k in range(KT):
                            terms += three(x_hi[:, k, r * P:(r + 1) * P], x_lo[:, k, r * P:(r + 1) * P],
                                           we_hi[:, k, :], we_lo[:, k, :])
                        last = products(ps, terms, *banks.free[i])
                        dve.wait(last, weighted)
                        t = dve.mark(V.scalar_tensor_tensor(out=residual[:, r, :], in0=ps, scalar=weight[:, r:r + 1],
                                                            in1=residual[:, r, :], op0=ALU.mult, op1=ALU.add))
                        banks.free[i] = (t,)
                        side.tick(2)
                    for r in range(RT):
                        i, ps = banks.next()
                        terms = []
                        for k in range(KT):
                            terms += three(h_hi[:, k, r * P:(r + 1) * P], h_lo[:, k, r * P:(r + 1) * P],
                                           wd_hi[:, k, :], wd_lo[:, k, :])
                        done = products(ps, terms, hidden, *banks.free[i])
                        dve.wait(done, t)
                        u = dve.mark(V.tensor_tensor(residual[:, r, :], ps, residual[:, r, :], ALU.add))
                        banks.free[i] = (u,)
                        side.tick(3)
                        if r == RT - 2 and more:
                            finish(operand(side.finish(), last))
                    store_rows(0, out, b, residual, u)
                    end_loop()

                core.dma(20, bo[:], a["bo1"].partition_broadcast(P))
                core.dma(20, gamma[:], a["gamma"].partition_broadcast(P))
                core.dma(20, beta[:], a["beta"].partition_broadcast(P))
                got = core.dma(20, rs[:], a["rs"].partition_broadcast(P))
                dve.wait(got)
                dve.mark(V.tensor_scalar(rs[:], rs[:], 0.0, 0.3, ALU.max, ALU.min))
                stage = Ring([residual[:, r, :] for r in range(RT)] +
                             [sbuf(scope, f"f1_stage{i}", [P, D]) for i in range(4)])
                w_hi, w_lo, _ = finish(load_split_weight(scope, "wo1", a["wo1_t"], stage, D))
                first = Side(projected(0))
                weights = []
                for name, dram, width in (("wu", a["wu_t"], D), ("wd", a["wd_t"], D), ("we", a["we"], D),
                                          ("wg", a["wg_t"], NE)):
                    part = Side(load_split_weight(scope, name, dram, stage, width))
                    while part.chain is not None:
                        part.tick()
                        first.tick()
                    weights.append(part.value)
                (wu_hi, wu_lo, _), (wd_hi, wd_lo, _), (we_hi, we_lo, _), (wg_hi, wg_lo, _) = weights
                finish(operand(first.finish()))
                core.fence()
                banks.reset()
                with nc.Fori(0, B - 1) as b:
                    batch(b, True)
                batch(B - 1, False)

        kv_and_q_projection()
        attention(0)
        out_projection_and_ffn_0()
        q_projection_1()
        attention(1)
        out_projection_and_ffn_1()


def laid_out(inputs):
    import numpy as np

    f = {k: np.asarray(v) for k, v in inputs.items()}
    c = np.ascontiguousarray
    columns = lambda v: c(v.reshape(KT, P).T)
    row = lambda v: c(v.reshape(-1))
    mask = np.pad(f["mask_BxS2_ik0"], ((0, 0), (0, TT * P - T)))
    return {
        "x": c(f["x"]), "ctx_t": c(f["ctx_2048"].transpose(0, 2, 1)),
        "mask_t": c(mask.reshape(B, TT, P).transpose(2, 0, 1)),
        "wq0": c(f["L0_xattn_wq"]), "bq0": columns(f["L0_xattn_bq"]),
        "wkv0_t": c(f["L0_xattn_wkv"].T),
        "bk0": columns(f["L0_xattn_bkv"][:D]), "bv0": row(f["L0_xattn_bkv"][D:]),
        "wp0": c(f["L0_xattn_wp"]), "bp0": row(f["L0_xattn_bp"]),
        "w1_t": c(f["L0_ffn_W1"].T), "w2_t": c(f["L0_ffn_W2"].T),
        "wq1_t": c(f["L1_xattn_Wq"].T), "bq1": columns(f["L1_xattn_bq"]),
        "wk1_t": c(f["L1_xattn_Wk"].T), "bk1": columns(f["L1_xattn_bk"]),
        "wv1_t": c(f["L1_xattn_Wv"].T), "bv1": row(f["L1_xattn_bv"]),
        "wo1_t": c(f["L1_xattn_Wo"].T), "bo1": row(f["L1_xattn_bo"]),
        "gamma": row(f["L1_xattn_ln_gamma"]), "beta": row(f["L1_xattn_ln_beta"]),
        "rs": c(f["L1_xattn_residual_scale"].reshape(1)),
        "wu_t": c(f["L1_ffn_W_up"].T), "wd_t": c(f["L1_ffn_W_down"].T),
        "wg_t": c(f["L1_ffn_W_gate"].T), "we": c(f["L1_ffn_W_expert"]),
    }


def kernel(**inputs):
    import concourse.bacc as bacc
    from concourse.bass_utils import run_bass_kernel_spmd

    nc = bacc.Bacc("TRN2", target_bir_lowering=False, num_devices=1)
    arrays = {f"in_{k}": v for k, v in laid_out(inputs).items()}
    args = {k[3:]: nc.dram_tensor(k, v.shape, mybir.dt.from_np(v.dtype), kind="ExternalInput").ap()
            for k, v in arrays.items()}
    result = nc.dram_tensor("result", (B, S, D), F32, kind="ExternalOutput").ap()
    build(nc, args, result)
    return run_bass_kernel_spmd(nc, [arrays], core_ids=[0]).results[0]["result"]
```

```python
from contextlib import ExitStack

import concourse.bass as bass
from concourse import mybir

F32 = mybir.dt.float32
F32R = mybir.dt.float32r
BF16 = mybir.dt.bfloat16
I32 = mybir.dt.int32
ALU = mybir.AluOpType
ACT = mybir.ActivationFunctionType
AX = mybir.AxisListType

P = 128
B, S, D, T, H, FF, NE = 4, 512, 512, 1601, 16, 2048, 8
DH = D // H
KT = D // P
RT = S // P
HPG = P // DH
NG = H // HPG
TT = -(-T // P)
TP = T + T % 2
TROWS = [min(P, T - P * i) for i in range(TT)]
KCH = [(0, 402), (402, 400), (802, 400), (1202, 400)]
MCH, MW, MV = [0, 400, 800, 1200], 402, 401
FT = FF // P
MAGIC = 12582912.0
ROOT = float(DH) ** 0.5
POOLED = ([0, 1, 3, 5, 7, 9, 11], [0, 1, 3, 5, 7, 9, 11])
FIRST_SUM = 2
LAG = 2
ORDER = (("scores", "tick", "values", "tick", "scores", "tick", "sums", "tick"),
         ("scores", "scores", "tick", "values", "tick", "tick", "sums", "tick"))
CLOSE = 8
PAUSE_Q0, PAUSE_O0, PAUSE_O1 = 12, 3, 2
STEPS_LOAD_0, STEPS_LOAD_1, STEPS_FFN_1, STEPS_LAST = 1, 3, 3, 3
EPS = 1e-5
EARLY = 23


class Lane:

    def __init__(self, engine, sem):
        self.e, self.sem, self.n, self.seen = engine, sem, 0, {}

    def wait(self, *tokens):
        for t in tokens:
            if t is None:
                continue
            sem, value, before = (*t, None)[:3]
            if self.seen.get(id(sem), 0 if before is None else -1) < value:
                self.e.wait_ge(sem, value if before is None else before + value)
                self.seen[id(sem)] = value

    def mark(self, instruction):
        instruction.then_inc(self.sem, 1)
        self.n += 1
        return self.sem, self.n


class Core:
    def __init__(self, nc, stack):
        self.nc = nc
        sem = lambda name: stack.enter_context(nc.semaphore(name))
        self.pe = Lane(nc.tensor, sem("pe_done"))
        self.act = Lane(nc.scalar, sem("act_done"))
        self.dve = Lane(nc.vector, sem("dve_done"))
        self.pool = Lane(nc.gpsimd, sem("pool_done"))
        self.sp = Lane(nc.sync, None)
        self.lanes = (self.pe, self.act, self.dve, self.pool, self.sp)
        self.dma_sems = [sem(f"dma_{i}") for i in range(24)]
        self.dma_count = {}
        self.kept = {}

    def keep(self, k, turn, per_turn):
        self.kept[k] = turn * (16 * per_turn) + 16
        self.dma_count[k] = 0
        return self.dma_sems[k], 0, self.kept[k]

    def release(self, k, total):
        del self.kept[k]
        self.dma_count[k] = 16 * total + 16

    def hold(self, k):
        self.kept[k] = self.dma_count[k] = 0

    def unhold(self, k, total):
        del self.kept[k]
        self.dma_count[k] = 16 * total
        return self.dma_sems[k], 16 * total

    def dma(self, k, dst, src, *tokens, lane=None):
        lane = lane or self.sp
        lane.wait(*tokens)
        dst, src = (x.bitcast(F32) if x.dtype == F32R else x for x in (dst, src))
        lane.e.dma_start(dst, src).then_inc(self.dma_sems[k], 16)
        self.dma_count[k] = self.dma_count.get(k, 0) + 16
        return (self.dma_sems[k], self.dma_count[k], *((self.kept[k],) if k in self.kept else ()))

    def fence(self):
        landed = {k: n for k, n in self.dma_count.items() if k not in self.kept}
        for k, n in landed.items():
            self.sp.wait((self.dma_sems[k], n))
        for lane in self.lanes[:4]:
            if lane.n:
                lane.wait((lane.sem, lane.n))
        self.nc.all_engine_barrier()
        for lane in self.lanes[:4]:
            if lane.n:
                lane.e.sem_clear(lane.sem)
        for k in landed:
            self.sp.e.sem_clear(self.dma_sems[k])
        self.nc.all_engine_barrier()
        for lane in self.lanes:
            lane.n, lane.seen = 0, {}
        self.dma_count = {k: self.dma_count[k] for k in self.kept}


class Ring:

    def __init__(self, buffers):
        self.buffers, self.free, self.at = buffers, [()] * len(buffers), -1

    def next(self):
        self.at = (self.at + 1) % len(self.buffers)
        return self.at, self.buffers[self.at]

    def reset(self):
        self.free, self.at = [()] * len(self.buffers), -1


def at(dram, i):
    if isinstance(i, int):
        return dram[i]
    names = "abcdef"[:len(dram.shape) - 1]
    return dram[bass.ds(i, 1)].rearrange(f"o {' '.join(names)} -> (o {names[0]}) {' '.join(names[1:])}")


def f32(ap):
    return ap.bitcast(F32)


def finish(chain):
    while True:
        try:
            next(chain)
        except StopIteration as end:
            return end.value


def together(*chains):
    values, live = [None] * len(chains), list(range(len(chains)))
    while live:
        for n in list(live):
            try:
                next(chains[n])
            except StopIteration as end:
                values[n] = end.value
                live.remove(n)
    return values


def pause(steps):
    for _ in range(steps):
        yield


class Side:

    def __init__(self, chain):
        self.chain, self.value = chain, None

    def tick(self, steps=1):
        for _ in range(steps):
            if self.chain is None:
                return
            try:
                next(self.chain)
            except StopIteration as end:
                self.value, self.chain = end.value, None

    def finish(self):
        while self.chain is not None:
            self.tick()
        return self.value


def build(nc, a, out):
    stack = ExitStack()
    with stack:
        core = Core(nc, stack)
        pe, act, dve, pool, sp = core.lanes
        V, A, M, G = nc.vector, nc.scalar, nc.tensor, nc.gpsimd

        psum = stack.enter_context(nc.psum_tensor("psum", [P, 8, 512], F32))
        bank = lambda i: psum[:, i, :]
        banks = Ring([bank(i) for i in range(8)])

        def sbuf(scope, name, shape, dt=F32):
            return scope.enter_context(nc.sbuf_tensor(name, shape, dt))

        ident = sbuf(stack, "ident", [P, P])
        minus_half = sbuf(stack, "minus_half", [P, RT])
        opening = sbuf(stack, "opening", [P, len(core.dma_sems)])

        def scratch(name, shape, dt=F32):
            return nc.dram_tensor(name, shape, dt).ap()

        k_hi = [scratch(f"k_hi{n}", (B * NG, P, TP)) for n in range(2)]
        k_lo = [scratch(f"k_lo{n}", (B * NG, P, TP)) for n in range(2)]
        v_rows = [scratch(f"v_rows{n}", (B, TT * P, D)) for n in range(2)]
        q_hi = [scratch(f"q_hi{n}", (B * NG, P, S)) for n in range(2)]
        q_lo = [scratch(f"q_lo{n}", (B * NG, P, S)) for n in range(2)]
        o_t = [scratch(f"o_t{n}", (1 + B * NG, P, S)) for n in range(2)]
        x_mid = [scratch(f"x_mid{n}", (B, S, D)) for n in range(3)]
        x_in = a["x"]

        t0 = pool.mark(G.memset(ident[:], 0.0))
        pool.wait(t0)
        pool.mark(G.affine_select(out=ident[:], in_=ident[:], compare_op=ALU.not_equal, fill=1.0,
                                  base=0, pattern=[[-1, P]], channel_multiplier=1))
        dve.mark(V.memset(minus_half[:], -0.5))
        core.fence()

        def open_kept(*ks):
            for k in ks:
                V.memset(opening[:, k:k + 1], 0.0).then_inc(core.dma_sems[k], 16)

        def split(hi, lo, src, *tokens, lane=dve):
            act.wait(*tokens)
            h = act.mark(A.activation(hi, src, ACT.Copy))
            lane.wait(h, *tokens)
            return lane.mark(lane.e.tensor_tensor(lo, src, f32(hi), ALU.subtract))

        def load_split_weight(scope, name, dram, stage, width):
            n = dram.shape[0] // P
            hi = sbuf(scope, f"{name}_hi", [P, n, width], F32R)
            lo = sbuf(scope, f"{name}_lo", [P, n, width], F32R)
            done, tile = {}, 0
            for k in range(n):
                for c in range(0, width, 512):
                    w = min(512, width - c)
                    i, buf = stage.next()
                    got = core.dma(i, buf[:, 0:w], dram[k * P:(k + 1) * P, c:c + w], *stage.free[i])
                    tile += 1
                    lane = pool if tile % 2 == 0 else dve
                    done[lane] = split(hi[:, k, c:c + w], lo[:, k, c:c + w], buf[:, 0:w], got, lane=lane)
                    stage.free[i] = (done[lane],)
                    yield
            return hi, lo, tuple(done.values())

        def products(dst, terms, *tokens):
            pe.wait(*tokens)
            for n, (lhs, rhs) in enumerate(terms):
                m = M.matmul(dst, lhs, rhs, start=(n == 0), stop=(n == len(terms) - 1))
            return pe.mark(m)

        def three(l_hi, l_lo, r_hi, r_lo):
            return [(l_hi, r_hi), (l_hi, r_lo), (l_lo, r_hi)]

        def layer_norm(rows, normed, small, *tokens):
            stats, mv, ve, r, t = small
            dve.wait(*tokens)
            for k in range(RT):
                s = dve.mark(V.bn_stats(stats[:, k, :], rows[:, k, :]))
            yield
            dve.wait(s)
            for k in range(RT):
                s = dve.mark(V.bn_aggr(mv[:, k, :], stats[:, k, :]))
            dve.wait(s)
            s = dve.mark(V.tensor_scalar(ve[:], mv[:, :, 1], EPS, None, ALU.add))
            yield
            pool.wait(s)
            s = pool.mark(G.tensor_tensor(r[:], ve[:], minus_half[:], ALU.pow))
            yield
            dve.wait(s)
            s = dve.mark(V.tensor_tensor(t[:], r[:], r[:], ALU.mult))
            dve.wait(s)
            s = dve.mark(V.tensor_tensor(t[:], t[:], ve[:], ALU.mult))
            dve.wait(s)
            s = dve.mark(V.tensor_scalar(t[:], t[:], -0.5, 1.5, ALU.mult, ALU.add))
            dve.wait(s)
            s = dve.mark(V.tensor_tensor(r[:], r[:], t[:], ALU.mult))
            dve.wait(s)
            for k in range(RT):
                s = dve.mark(V.tensor_scalar(normed[:, k, :], rows[:, k, :], mv[:, k, 0:1], r[:, k:k + 1],
                                             ALU.subtract, ALU.mult))
                if k % 2:
                    yield
            return s

        def norm_small(scope, tag):
            return (sbuf(scope, f"stats_{tag}", [P, RT, 6]), sbuf(scope, f"mv_{tag}", [P, RT, 2]),
                    sbuf(scope, f"ve_{tag}", [P, RT]), sbuf(scope, f"r_{tag}", [P, RT]),
                    sbuf(scope, f"t_{tag}", [P, RT]))

        def quantise(rows, scale, recip, *tokens):
            dve.wait(*tokens)
            s = dve.mark(V.tensor_reduce(scale[:], rows[:], AX.X, ALU.max, apply_absolute_value=True))
            yield
            dve.wait(s)
            s = dve.mark(V.tensor_scalar(scale[:], scale[:], 1.0 / 127.0, 1e-8, ALU.mult, ALU.max))
            dve.wait(s)
            s = dve.mark(V.reciprocal(recip[:], scale[:]))
            dve.wait(s)
            for k in range(RT):
                s = dve.mark(V.tensor_scalar(rows[:, k, :], rows[:, k, :], recip[:, k:k + 1], 127.0,
                                             ALU.mult, ALU.min))
            yield
            dve.wait(s)
            s = dve.mark(V.tensor_scalar(rows[:], rows[:], -127.0, MAGIC, ALU.max, ALU.add))
            yield
            dve.wait(s)
            s = dve.mark(V.tensor_scalar(rows[:], rows[:], MAGIC, None, ALU.subtract))
            yield
            return s

        def transposed(rows, use, *tokens, ring=banks):
            for k in range(KT):
                i, dst = ring.next()
                pe.wait(*ring.free[i], *tokens)
                for r in range(RT):
                    m = M.transpose(dst[:, r * P:(r + 1) * P], rows[:, r, k * P:(k + 1) * P], ident[:])
                done = use(k, dst, pe.mark(m))
                ring.free[i] = (done,)
                yield
            return done

        def load_rows(k, dst, dram, i, *tokens):
            return core.dma(k, dst[:], at(dram, i).rearrange("(r p) d -> p r d", p=P), *tokens)

        def store_rows(k, dram, i, src, *tokens):
            return core.dma(k, at(dram, i).rearrange("(r p) d -> p r d", p=P), src[:], *tokens)

        def quantised_weight(scope, name, dram, stage_rows, dma, ring=banks):
            wt = sbuf(scope, f"{name}_t", [P, KT, D], BF16)
            scale = sbuf(scope, f"{name}_scale", [P, KT])
            recip = sbuf(scope, f"{name}_recip", [P, KT])
            got = core.dma(dma, stage_rows[:], dram.rearrange("(r p) d -> p r d", p=P))
            q = yield from quantise(stage_rows, scale, recip, got)

            def keep(k, src, token):
                act.wait(token)
                return act.mark(A.activation(wt[:, k, :], src, ACT.Copy))
            token = yield from transposed(stage_rows, keep, q, ring=ring)
            return wt, scale, token

        def row_of(dst, columns, *tokens, ring=banks):
            i, ps = ring.next()
            pe.wait(*ring.free[i], *tokens)
            for r in range(RT):
                m = M.matmul(ps[:, r * P:(r + 1) * P], columns[:, r:r + 1].to_broadcast([P, P]), ident[:],
                             start=True, stop=True)
            token = pe.mark(m)
            act.wait(token)
            ring.free[i] = (act.mark(A.activation(dst, ps, ACT.Copy)),)
            return ring.free[i][0]

        def start_loop():
            core.fence()
            banks.reset()

        def end_loop():
            core.fence()
            banks.reset()

        def store_q(n, b, g, parts, token, k):
            core.dma(k, at(q_hi[n], b * NG + g), parts[0][:], token)
            return core.dma(k, at(q_lo[n], b * NG + g), parts[1][:], token)

        def kv_and_q_projection():
            with ExitStack() as scope:
                raw = [sbuf(scope, f"ctx_raw{k}", [P, T]) for k in range(KT)]
                v_out = [sbuf(scope, f"v_out{i}", [P, D]) for i in range(4)]
                spare = [sbuf(scope, "q0_full", [P, S]), sbuf(scope, "q0_step_row", [P, S])]
                stage = Ring([buf[:] for buf in v_out + spare])
                rows = sbuf(scope, "q0_rows", [P, RT, D])
                small = norm_small(scope, "q0")
                step = sbuf(scope, "q0_step", [P, RT])
                recip = sbuf(scope, "q0_recip", [P, RT])
                xq_t = sbuf(scope, "q0_xq_t", [P, KT, S], BF16)
                bq = sbuf(scope, "q0_bq", [P, KT])
                full, step_row = spare
                parts = [sbuf(scope, f"q0_part{j}", [P, S], F32R) for j in range(2)]
                QUANTISED = 8
                LOADED = 16
                wq = Side(quantised_weight(scope, "wq0", a["wq0"], rows, QUANTISED))
                core.dma(QUANTISED + 1, bq[:], a["bq0"])
                wk, wv, bk, bv = [], [], [], []
                for n, (kd, vd) in enumerate(((a["wkv0_t"][:, 0:D], a["wkv0_t"][:, D:2 * D]),
                                              (a["wk1_t"], a["wv1_t"]))):
                    for kept, name, dram in ((wk, f"wk{n}", kd), (wv, f"wv{n}", vd)):
                        weight = Side(load_split_weight(scope, name, dram, stage, D))
                        while weight.chain is not None:
                            weight.tick()
                            wq.tick()
                        kept.append(weight.value)
                    bk.append(sbuf(scope, f"bk{n}", [P, KT]))
                    bv.append(sbuf(scope, f"bv{n}", [P, D]))
                    core.dma(QUANTISED + 2, bk[n][:], a[f"bk{n}"])
                    core.dma(QUANTISED + 2, bv[n][:], a[f"bv{n}"].partition_broadcast(P))
                wt, w_step, _ = wq.finish()
                c_hi = sbuf(scope, "ctx_hi", [P, KT, TP], F32R)
                c_lo = sbuf(scope, "ctx_lo", [P, KT, TP], F32R)
                kt_hi = [sbuf(scope, f"kt_hi{i}", [P, TP], F32R) for i in range(2)]
                kt_lo = [sbuf(scope, f"kt_lo{i}", [P, TP], F32R) for i in range(2)]
                dve.mark(V.memset(f32(c_hi[:, :, T:TP]), 0.0))
                dve.mark(V.memset(f32(c_lo[:, :, T:TP]), 0.0))

                def q_of(b):
                    got = load_rows(QUANTISED, rows, x_in, b)
                    yield from pause(3)
                    s = yield from layer_norm(rows, rows, small, got)
                    s = yield from quantise(rows, step, recip, s)
                    yield from pause(PAUSE_Q0)
                    stepped = row_of(step_row[:], step, s)
                    yield

                    def keep(k, src, token):
                        act.wait(token)
                        return act.mark(A.activation(xq_t[:, k, :], src, ACT.Copy))
                    ready = yield from transposed(rows, keep, s)
                    yield
                    free = ()
                    for g in range(NG):
                        i, ps = banks.next()
                        done = products(ps, [(wt[:, k, g * P:(g + 1) * P], xq_t[:, k, :]) for k in range(KT)],
                                        ready, *banks.free[i])
                        dve.wait(done, stepped, *free)
                        t = dve.mark(V.scalar_tensor_tensor(out=full[:], in0=ps, scalar=w_step[:, g:g + 1],
                                                            in1=step_row[:], op0=ALU.mult, op1=ALU.mult))
                        banks.free[i] = (t,)
                        dve.wait(t)
                        h = dve.mark(V.tensor_scalar(parts[0][:], full[:], bq[:, g:g + 1], None, ALU.add))
                        dve.wait(h)
                        l = dve.mark(V.scalar_tensor_tensor(out=parts[1][:], in0=full[:], scalar=bq[:, g:g + 1],
                                                            in1=f32(parts[0][:]), op0=ALU.add, op1=ALU.subtract))
                        free = (store_q(0, b, g, parts, l, QUANTISED + 1), l)
                        yield
                        yield

                def load_context(b, k, *tokens):
                    core.dma(LOADED + k, raw[k][:], at(a["ctx_t"], b)[k * P:(k + 1) * P, :], *tokens)

                def k_terms(n, g, k, c0, cw):
                    w_hi, w_lo, _ = wk[n]
                    return three(w_hi[:, k, g * P:(g + 1) * P], w_lo[:, k, g * P:(g + 1) * P],
                                 c_hi[:, k, c0:c0 + cw], c_lo[:, k, c0:c0 + cw])

                def batch(b, more):
                    side = Side(q_of(b))
                    ready = [[split(c_hi[:, k, c0:min(c0 + cw, T)], c_lo[:, k, c0:min(c0 + cw, T)],
                                    raw[k][:, c0:min(c0 + cw, T)]) for c0, cw in KCH] for k in range(KT)]
                    opened = []
                    for c0, cw in KCH:
                        opened.append(banks.next())
                    for k in range(KT):
                        for (i, ps), (c0, cw), part in zip(opened, KCH, ready[k]):
                            pe.wait(part)
                            for m_, (lhs, rhs) in enumerate(k_terms(0, 0, k, c0, cw)):
                                m = M.matmul(ps[:, 0:cw], lhs, rhs, start=(k == 0 and m_ == 0),
                                             stop=(k == KT - 1 and m_ == 2))
                            done = pe.mark(m)
                    first_done = done
                    kt_free = [(), ()]
                    v_free = [(core.keep(12 + s, b, len(range(s, 2 * TT, 4))),) for s in range(4)]
                    nk = nv = 0
                    for n in range(2):
                        for g in range(NG):
                            s = nk % 2
                            nk += 1
                            for c, (c0, cw) in enumerate(KCH):
                                if n == g == 0:
                                    (i, ps), done = opened[c], first_done
                                else:
                                    i, ps = banks.next()
                                    terms = []
                                    for k in range(KT):
                                        terms += k_terms(n, g, k, c0, cw)
                                    done = products(ps[:, 0:cw], terms, *banks.free[i])
                                act.wait(done, *kt_free[s])
                                h = act.mark(A.activation(kt_hi[s][:, c0:c0 + cw], ps[:, 0:cw], ACT.Identity,
                                                          bias=bk[n][:, g:g + 1]))
                                dve.wait(h, *kt_free[s])
                                banks.free[i] = (dve.mark(V.scalar_tensor_tensor(
                                    out=kt_lo[s][:, c0:c0 + cw], in0=ps[:, 0:cw], scalar=bk[n][:, g:g + 1],
                                    in1=f32(kt_hi[s][:, c0:c0 + cw]), op0=ALU.add, op1=ALU.subtract)),)
                                if not n == g == 0:
                                    side.tick()
                            core.dma(4 + s, at(k_hi[n], b * NG + g), kt_hi[s][:], h)
                            kt_free[s] = (core.dma(4 + s, at(k_lo[n], b * NG + g), kt_lo[s][:],
                                                   *banks.free[i]),)
                            if more and n == 0:
                                load_context(b + 1, g, ready[g][-1])
                        w_hi, w_lo, _ = wv[n]
                        for t, height in enumerate(TROWS):
                            s = nv % 4
                            nv += 1
                            i, ps = banks.next()
                            terms = []
                            for k in range(KT):
                                terms += three(c_hi[:, k, t * P:t * P + height], c_lo[:, k, t * P:t * P + height],
                                               w_hi[:, k, :], w_lo[:, k, :])
                            done = products(ps[0:height, :], terms, *banks.free[i])
                            dve.wait(done, *v_free[s])
                            banks.free[i] = (dve.mark(V.tensor_tensor(v_out[s][0:height, :], ps[0:height, :],
                                                                      bv[n][0:height, :], ALU.add)),)
                            v_free[s] = (core.dma(12 + s, at(v_rows[n], b)[t * P:t * P + height, :],
                                                  v_out[s][0:height, :], *banks.free[i]),)
                            side.tick()
                    side.finish()
                    end_loop()

                for k in range(KT):
                    load_context(0, k)
                start_loop()
                open_kept(12, 13, 14, 15)
                with nc.Fori(0, B - 1) as b:
                    batch(b, True)
                batch(B - 1, False)
                for s in range(4):
                    core.release(12 + s, B * len(range(s, 2 * TT, 4)))
                core.fence()

        def early_part(k_slot, v_slot, turn):
            yield from pause(2)
            half = bass.ds(turn * (TP // 2), TP // 2)
            for quarter in range(4):
                core.dma(EARLY, k_slot[quarter * DH:(quarter + 1) * DH, :, half],
                         (k_hi, k_lo)[quarter % 2][1][0][:, half].rearrange("(j d) t -> d j t", d=DH))
                yield
            half = (TT - 1) // 2
            core.dma(EARLY, v_slot[:, bass.ds(turn * half, half), :],
                     v_rows[1][0][bass.ds(turn * (half * P), half * P), 0:P].rearrange("(t p) c -> p t c", p=P))

        def q_projection_1(early):
            with ExitStack() as scope:
                bq = sbuf(scope, "q1_bq", [P, KT])
                stage = Ring([sbuf(scope, f"q1_stage{i}", [P, 512]) for i in range(4)])
                w_hi, w_lo, _ = finish(load_split_weight(scope, "wq1", a["wq1_t"], stage, D))
                core.dma(5, bq[:], a["bq1"])

                def slot(n):
                    return (sbuf(scope, f"q1_rows{n}", [P, RT, D]), norm_small(scope, f"q1_{n}"),
                            sbuf(scope, f"q1_x_hi{n}", [P, KT, S], F32R), sbuf(scope, f"q1_x_lo{n}", [P, KT, S], F32R),
                            [[sbuf(scope, f"q1_part{n}{i}{j}", [P, S], F32R) for j in range(2)] for i in range(2)])

                def q_of(b, turn, buffers, dma):
                    rows, small, x_hi, x_lo, parts = buffers
                    got = load_rows(dma, rows, x_mid[1], b)
                    yield
                    s = yield from layer_norm(rows, rows, small, got)
                    ready = yield from transposed(
                        rows, lambda k, src, t: split(x_hi[:, k, :], x_lo[:, k, :], src, t), s)
                    free = [(core.keep(dma + 1 + i, turn, NG),) for i in range(2)]
                    for g in range(NG):
                        i, ps = banks.next()
                        terms = []
                        for k in range(KT):
                            terms += three(w_hi[:, k, g * P:(g + 1) * P], w_lo[:, k, g * P:(g + 1) * P],
                                           x_hi[:, k, :], x_lo[:, k, :])
                        done = products(ps, terms, ready, *banks.free[i])
                        hi, lo = parts[g % 2]
                        act.wait(done, *free[g % 2])
                        h = act.mark(A.activation(hi[:], ps, ACT.Identity, bias=bq[:, g:g + 1]))
                        dve.wait(h, *free[g % 2])
                        l = dve.mark(V.scalar_tensor_tensor(out=lo[:], in0=ps, scalar=bq[:, g:g + 1],
                                                            in1=f32(hi[:]), op0=ALU.add, op1=ALU.subtract))
                        banks.free[i] = (l,)
                        free[g % 2] = (store_q(1, b, g, (hi, lo), l, dma + 1 + g % 2),)
                        yield

                slots = [slot(n) for n in range(2)]
                start_loop()
                stores = [8 * n + 1 + i for n in range(2) for i in range(2)]
                open_kept(*stores)
                core.hold(EARLY)
                core.dma(EARLY, early[1][0:TROWS[-1], TT - 1, :], v_rows[1][0][(TT - 1) * P:T, 0:P])
                with nc.Fori(0, B // 2) as pair:
                    together(*[q_of(pair * 2 + n, pair, slots[n], 8 * n) for n in range(2)],
                             early_part(*early, pair))
                    end_loop()
                for k in stores:
                    core.release(k, B // 2 * NG)
                core.fence()

        def attention(n, early=None):
            first = n == 0
            pooled_tiles = POOLED[n]
            NQ = 3 if first else 4
            with ExitStack() as scope:
                k_st = [sbuf(scope, f"k_st{n}{s}", [P, HPG, TP], F32R) if s or first else early[0]
                        for s in range(NG)]
                q_st = [sbuf(scope, f"q_st{n}{s}", [P, HPG, S], F32R) for s in range(NG)]
                v_st = [sbuf(scope, f"v_st{n}{s}", [P, TT, P]) if s or first else early[1] for s in range(2)]
                probs = Ring([sbuf(scope, f"probs{n}{i}", [P, HPG, S]) for i in range(5)])
                pooled = sbuf(scope, f"pooled{n}", [P, HPG, S])
                ones = sbuf(scope, f"ones{n}", [P, DH])
                acc_sb = sbuf(scope, f"acc_sb{n}", [P, S])
                den_sb = sbuf(scope, f"den_sb{n}", [P, S])
                rec = sbuf(scope, f"rec{n}", [P, RT * HPG])
                unity = sbuf(scope, f"unity{n}", [P, RT * HPG])
                o_sb = sbuf(scope, f"o_sb{n}", [P, S])
                W = 2
                scores = windows = Ring([psum[:, 2 * i:2 * i + 2, :] for i in range(3)])
                acc, den = bank(6), bank(7)
                dve.mark(V.memset(ones[:], 1.0))
                dve.mark(V.memset(den_sb[:], 1.0))
                dve.mark(V.memset(acc_sb[:], 0.0))
                if first:
                    neg_max = sbuf(scope, "neg_max", [P, HPG, RT, DH])
                    win_max = sbuf(scope, "win_max", [P, HPG, RT, 2])
                    max_hi = sbuf(scope, "max_hi", [P, HPG, RT], F32R)
                    dve.mark(V.memset(neg_max[:], 0.0))
                    dve.mark(V.memset(f32(k_st[0][96:128, :, :]), 1.0))
                    for s in range(1, NG):
                        pool.mark(G.memset(f32(k_st[s][96:128, :, :]), 1.0))
                else:
                    mask_i = sbuf(scope, "mask_i", [P, B, TT], I32)
                    bound = sbuf(scope, "bound", [P, B, TT])
                    top = sbuf(scope, "top", [P, TT])
                    got = core.dma(9, mask_i[:], a["mask_t"])
                    dve.wait(got)
                    s_ = dve.mark(V.tensor_scalar(bound[:], mask_i[:], 0.5, 100.0 * ROOT, ALU.is_gt, ALU.mult))
                    dve.wait(s_)
                    dve.mark(V.tensor_scalar(bound[:], bound[:], 50.0 * ROOT, None, ALU.subtract))

                loaded = {}

                def load(s, unit, *tokens, with_k=True):
                    sp.wait(*tokens)
                    for quarter in range(NQ):
                        rows = slice(quarter * DH, (quarter + 1) * DH)
                        k_src = (k_hi, k_lo, k_hi, k_lo)[quarter][n]
                        q_src = (q_hi, q_hi, q_lo, q_lo)[quarter][n]
                        if with_k:
                            core.dma(s, k_st[s][rows, :, :], at(k_src, unit).rearrange("(j d) t -> d j t", d=DH))
                        loaded[s] = core.dma(s, q_st[s][rows, :, :],
                                             at(q_src, unit).rearrange("(j d) t -> d j t", d=DH))

                def load_v(b, g, *tokens):
                    s = g % 2
                    v_src = at(v_rows[n], b)[:, g * P:(g + 1) * P]
                    core.dma(4 + s, v_st[s][:, 0:TT - 1, :],
                             v_src[0:(TT - 1) * P, :].rearrange("(t p) c -> p t c", p=P), *tokens)
                    loaded[4 + s] = core.dma(4 + s, v_st[s][0:TROWS[-1], TT - 1, :], v_src[(TT - 1) * P:T, :])

                def max_pass(s):
                    pieces, done = [], {}

                    def window(j, r, c):
                        i, ps = windows.next()
                        pe.wait(loaded.get(s), *windows.free[i])
                        for w in range(2):
                            start = MCH[2 * c + w]
                            m = M.matmul(ps[:, w, 0:MW], q_st[s][0:96, j, r * P:(r + 1) * P],
                                         k_st[s][0:96, j, start:start + MW], start=True, stop=True)
                        m = pe.mark(m)
                        dve.wait(m)
                        done[j] = dve.mark(V.tensor_reduce(win_max[:, j, r, c:c + 1], ps[:, :, 0:MV], AX.XY, ALU.max))
                        windows.free[i] = (done[j],)

                    def columns(j):
                        two = slice(j, j + 2)
                        dve.wait(done[j + 1])
                        t = dve.mark(V.tensor_reduce(neg_max[:, two, :, 0], win_max[:, two, :, :], AX.X, ALU.max,
                                                     negate=True))
                        dve.wait(t)
                        t = dve.mark(V.tensor_copy(max_hi[:, two, :], neg_max[:, two, :, 0]))
                        dve.wait(t)
                        done[j] = dve.mark(V.tensor_tensor(neg_max[:, two, :, 1], neg_max[:, two, :, 0],
                                                           f32(max_hi[:, two, :]), ALU.subtract))

                    def turn(j):
                        i, ps = windows.next()
                        pe.wait(done[j], *windows.free[i])
                        for jj in range(2):
                            for r in range(RT):
                                m = M.matmul(ps[96:128, jj, r * P:(r + 1) * P], neg_max[:, j + jj, r, :], ident[:],
                                             start=True, stop=True)
                        t = pe.mark(m)
                        dve.wait(t)
                        max_ready[s] = dve.mark(V.tensor_copy(q_st[s][96:128, j:j + 2, :], ps[96:128, :, :]))
                        windows.free[i] = (max_ready[s],)

                    for j in range(HPG):
                        for r in range(RT):
                            for c in range(2):
                                pieces.append(lambda j=j, r=r, c=c: window(j, r, c))
                                if j == 2 and r == 1 and c == 0:
                                    pieces.append(lambda: turn(0))
                        if j % 2:
                            pieces.append(lambda j=j: columns(j - 1))
                    pieces.append(lambda: None)
                    pieces.append(lambda: turn(2))
                    return pieces

                max_ready = {}
                state = {}

                tiles = {}

                def begin(g, t):
                    pi, pr = probs.next()
                    tiles[g, t] = [pi, pr, [], probs.free[pi], 0]
                    probs.free[pi] = ()

                def score(g, t, j):
                    rows = TROWS[t]
                    pi, pr, done, buffer_free, _ = tiles[g, t]
                    i, ps = scores.next()
                    pe.wait(loaded.get(g), max_ready.get(g), *scores.free[i])
                    for w in range(W):
                        m = M.matmul(ps[0:rows, w, :], k_st[g][:, j + w, t * P:t * P + rows],
                                     q_st[g][:, j + w, :], start=True, stop=True)
                    m = state["scored"] = pe.mark(m)
                    dst = pr[0:rows, j:j + W, :]
                    if first:
                        act.wait(m, *buffer_free)
                        e = act.mark(A.activation(dst, ps[0:rows], ACT.Exp, scale=1.0 / ROOT))
                        scores.free[i] = (e,)
                    else:
                        dve.wait(m, *buffer_free)
                        c = dve.mark(V.tensor_scalar(dst, ps[0:rows], top[0:rows, t:t + 1], -50.0 * ROOT,
                                                     ALU.min, ALU.max))
                        scores.free[i] = (c,)
                        act.wait(c)
                        e = act.mark(A.activation(dst, dst, ACT.Exp, scale=1.0 / ROOT))
                    done.append(e)

                def pool_sum(g, t):
                    k = pooled_tiles.index(t) if t in pooled_tiles else 0
                    if not k:
                        return
                    before = tiles[g, pooled_tiles[0]] if k == 1 else None
                    pool.wait(*tiles[g, t][2], state.get("pool"), *(state.get("pooled_free", ()) if k == 1 else ()))
                    state["pool"] = pool.mark(G.tensor_tensor(pooled[:], before[1][:] if before else pooled[:],
                                                              tiles[g, t][1][:], ALU.add))
                    probs.free[tiles[g, t][0]] += (state["pool"],)
                    if before:
                        probs.free[before[0]] += (state["pool"],)

                def values(g, t):
                    rows = TROWS[t]
                    pi, pr, done, _, _ = tiles[g, t]
                    pe.wait(*done, loaded.get(4 + g % 2))
                    if t == 0:
                        pe.wait(*state.get("acc_free", ()))
                    for j in range(HPG):
                        m = M.matmul(acc[j * DH:(j + 1) * DH, :], v_st[g % 2][0:rows, t, j * DH:(j + 1) * DH],
                                     pr[0:rows, j, :], start=(t == 0), stop=(t == TT - 1))
                    probs.free[pi] += (pe.mark(m),)

                def sums(g, t):
                    if t not in pooled_tiles:
                        rows = TROWS[t]
                        pi, pr, done, _, _ = tiles[g, t]
                        for j in range(HPG):
                            m = M.matmul(den[j * DH:(j + 1) * DH, :], ones[0:rows, :], pr[0:rows, j, :],
                                         start=(t == FIRST_SUM), stop=False)
                        probs.free[pi] += (pe.mark(m),)
                    if t == TT - 1:
                        pe.wait(state["pool"])
                        for j in range(HPG):
                            m = M.matmul(den[j * DH:(j + 1) * DH, :], ones[:], pooled[:, j, :],
                                         start=False, stop=True)
                        state["summed"] = pe.mark(m)
                        state["pooled_free"] = (state["summed"],)

                def normalise(entry):
                    def copy_out():
                        act.wait(state["summed"], *state.get("den_free", ()), *state.get("acc_sb_free", ()))
                        c = act.mark(A.activation(acc_sb[:], acc, ACT.Copy))
                        d = act.mark(A.activation(den_sb[:], den, ACT.Copy))
                        state["acc_free"], state["den_out"] = (c,), (d,)

                    def compact():
                        i, ps = scores.next()
                        pe.wait(*state.get("den_out", ()), *scores.free[i])
                        for q in range(RT):
                            m = M.matmul(ps[:, 0, q * HPG:(q + 1) * HPG], den_sb[:, q * P:(q + 1) * P],
                                         ident[:, 0:P:DH], start=True, stop=True)
                        m = pe.mark(m)
                        state["den_free"] = (m,)
                        dve.wait(m)
                        den_cols = ps[:, 0, 0:RT * HPG]
                        r = dve.mark(V.reciprocal(rec[:], den_cols))
                        if not first:
                            dve.wait(r)
                            r = dve.mark(V.scalar_tensor_tensor(out=unity[:], in0=den_cols, scalar=-1.0, in1=rec[:],
                                                                op0=ALU.mult, op1=ALU.mult))
                            dve.wait(r)
                            r = dve.mark(V.scalar_tensor_tensor(out=rec[:], in0=unity[:], scalar=2.0 - 1e-8,
                                                                in1=rec[:], op0=ALU.add, op1=ALU.mult))
                        scores.free[i] = (r,)
                        state["inverse"] = r

                    def scaled():
                        i, ps = scores.next()
                        pe.wait(state["inverse"], *scores.free[i])
                        for q in range(RT):
                            for j in range(HPG):
                                m = M.matmul(ps[j * DH:(j + 1) * DH, 0, q * P:(q + 1) * P],
                                             rec[:, q * HPG + j:q * HPG + j + 1].to_broadcast([P, DH]),
                                             ident[:], start=True, stop=True)
                        dve.wait(pe.mark(m), *state.get("acc_free", ()), *state.get("o_free", ()))
                        o = dve.mark(V.tensor_tensor(o_sb[:], acc_sb[:], ps[:, 0, :], ALU.mult))
                        scores.free[i] = (o,)
                        state["acc_sb_free"] = (o,)
                        state["o_free"] = (core.dma(8, at(o_t[n], entry), o_sb[:], o),)

                    return [(0, copy_out), (CLOSE, compact), (CLOSE, scaled)]

                def run_all(pieces):
                    for piece in pieces:
                        piece()

                AHEAD = 2 if first else 1

                def batch(b, more):
                    if not first:
                        top_ready = dve.mark(V.tensor_copy(top[:], bound[:, b, :] if isinstance(b, int) else
                                                           bound[:, bass.ds(b, 1), :].rearrange("p o t -> p (o t)")))
                        dve.wait(top_ready)
                    tiles.clear()
                    state["o_free"] = (core.keep(8, b, NG),)
                    load_v(b, 1)
                    todo, total, ran, scored = [], [0], [0, 0], {}
                    closing = normalise(b * NG)[1:]

                    def tick():
                        ran[0] += 1
                        if closing and ran[1] + closing[0][0] <= 0:
                            closing.pop(0)[1]()
                            ran[1] = 0
                        ran[1] -= 1
                        while todo and (total[0] - len(todo)) * (4 * TT - 2) < total[0] * ran[0] :
                            todo.pop(0)()

                    for step in range(NG * TT + LAG):
                        g, t = divmod(step, TT)
                        vg, vt = divmod(step - LAG, TT)
                        if g < NG and t == 0:
                            run_all(todo)
                            todo[:] = max_pass((g + 1) % NG) if first and (g + 1 < NG or more) else []
                            total[0], ran[0] = len(todo), 0
                            ahead = g + AHEAD
                            if ahead < NG or more:
                                nb = b if ahead < NG else b + 1
                                load(ahead % NG, nb * NG + ahead % NG, scored.get(ahead - NG))
                        if g < NG:
                            begin(g, t)
                        for part in ORDER[n]:
                            if part == "tick":
                                tick()
                            elif part == "scores" and g < NG:
                                score(g, t, tiles[g, t][4])
                                tiles[g, t][4] += W
                            elif part == "values" and step >= LAG:
                                values(vg, vt)
                            elif part == "sums" and step >= LAG:
                                if vt == FIRST_SUM:
                                    pe.wait(*state.get("den_out", ()))
                                sums(vg, vt)
                                if vt == TT - 1:
                                    if vg + 2 < NG or (vg + 2 == NG and more):
                                        load_v(b if vg + 2 < NG else b + 1, (vg + 2) % NG, state["summed"])
                                    closing[:] = normalise(b * NG + vg + 1)
                                    closing.pop(0)[1]()
                                    ran[1] = 0
                        if g < NG:
                            pool_sum(g, t)
                            if t == TT - 1:
                                scored[g] = state["scored"]
                    run_all(todo)
                    if not more:
                        run_all(piece for _, piece in closing)

                def reset():
                    core.fence()
                    for ring in (probs, scores):
                        ring.reset()
                    loaded.clear()
                    max_ready.clear()
                    state.clear()

                load(0, 0, with_k=first)
                if first:
                    load_v(0, 0)
                    load(1, 1)
                else:
                    sp.wait(core.unhold(EARLY, 2 * 5 + 1))
                if first:
                    pe.wait((dve.sem, dve.n))
                    run_all(max_pass(0))
                reset()
                open_kept(8)
                with nc.Fori(0, B - 1) as b:
                    batch(b, True)
                    reset()
                batch(B - 1, False)
                core.release(8, B * NG + 1)
                reset()
                banks.reset()

        def out_projection_and_ffn_0():
            with ExitStack() as scope:
                rows = sbuf(scope, "f0_rows", [P, RT, D])
                cols = sbuf(scope, "f0_cols", [P, RT, D])
                o_rows = sbuf(scope, "o0_rows", [P, RT, D])
                step = sbuf(scope, "o0_step", [P, RT])
                recip = sbuf(scope, "o0_recip", [P, RT])
                oq_t = sbuf(scope, "o0_oq_t", [P, KT, S], BF16)
                w_row = sbuf(scope, "o0_w_row", [P, D])
                bp = sbuf(scope, "o0_bp", [P, D])
                y = [sbuf(scope, f"o0_y{i}", [P, D]) for i in range(2)]
                residual = sbuf(scope, "f0_residual", [P, RT, D])
                code = [sbuf(scope, f"f0_code{i}", [P, S]) for i in range(2)]
                small = norm_small(scope, "f0")
                x_hi = sbuf(scope, "f0_x_hi", [P, KT, S], F32R)
                x_lo = sbuf(scope, "f0_x_lo", [P, KT, S], F32R)
                g_hi = [sbuf(scope, f"f0_g_hi{i}", [P, S], F32R) for i in range(2)]
                g_lo = [sbuf(scope, f"f0_g_lo{i}", [P, S], F32R) for i in range(2)]
                hidden = Ring([bank(i) for i in range(4)])
                PROJECTION = 8

                def projected(b, *tokens):
                    for g in range(NG):
                        got = core.dma(PROJECTION, cols[:, g, :], at(o_t[0], b * NG + g + 1), *tokens)
                    got_x = load_rows(PROJECTION + 1, rows, x_in, b, *tokens)
                    yield

                    def keep_rows(k, src, token):
                        act.wait(token)
                        return act.mark(A.activation(o_rows[:, k, :], src, ACT.Copy))
                    s = yield from transposed(cols, keep_rows, got, ring=hidden)
                    s = yield from quantise(o_rows, step, recip, s)
                    yield from pause(PAUSE_O0)

                    def keep(k, src, token):
                        act.wait(token)
                        return act.mark(A.activation(oq_t[:, k, :], src, ACT.Copy))
                    ready = yield from transposed(o_rows, keep, s, ring=hidden)
                    yield
                    free = [(), ()]
                    for r in range(RT):
                        i, ps = hidden.next()
                        done = products(ps, [(oq_t[:, k, r * P:(r + 1) * P], wt[:, k, :]) for k in range(KT)],
                                        ready, *hidden.free[i])
                        dve.wait(done, *free[r % 2])
                        t = dve.mark(V.scalar_tensor_tensor(out=y[r % 2][:], in0=ps, scalar=step[:, r:r + 1],
                                                            in1=w_row[:], op0=ALU.mult, op1=ALU.mult))
                        hidden.free[i] = (t,)
                        dve.wait(t, got_x)
                        t = dve.mark(V.tensor_tensor(y[r % 2][:], y[r % 2][:], bp[:], ALU.add))
                        dve.wait(t)
                        t = dve.mark(V.tensor_tensor(rows[:, r, :], rows[:, r, :], y[r % 2][:], ALU.add))
                        free[r % 2] = (t,)
                        yield
                    return (yield from layer_norm(rows, cols, small, t))

                def operand(s, *tokens):
                    return transposed(cols, lambda k, src, t: split(x_hi[:, k, :], x_lo[:, k, :], src, t, *tokens),
                                      s, ring=hidden)

                def batch(b, more):
                    side = Side(iter(()))
                    act.wait(core.keep(0, b, 1))
                    for r in range(RT):
                        copied = act.mark(A.activation(residual[:, r, :], rows[:, r, :], ACT.Copy))
                    if more:
                        side = Side(projected(b + 1, copied))
                    freed, made, last = {}, {}, {}

                    def first_half(f):
                        i, ps = hidden.next()
                        terms = []
                        for k in range(KT):
                            terms += three(w1_hi[:, k, f * P:(f + 1) * P], w1_lo[:, k, f * P:(f + 1) * P],
                                           x_hi[:, k, :], x_lo[:, k, :])
                        done = products(ps, terms, *hidden.free[i])
                        last["x"] = done
                        q = code[f % 2]
                        dve.wait(done, *freed.get(f - 2, ()))
                        t = dve.mark(V.tensor_scalar(q[:], ps, 10.0, -32768.0, ALU.mult, ALU.max))
                        hidden.free[i] = (t,)
                        dve.wait(t)
                        t = dve.mark(V.tensor_scalar(q[:], q[:], 32767.0, MAGIC, ALU.min, ALU.add))
                        dve.wait(t)
                        t = dve.mark(V.tensor_scalar(q[:], q[:], MAGIC, 0.1, ALU.subtract, ALU.mult))
                        act.wait(t, *freed.get(f - 2, ()))
                        t = act.mark(A.activation(q[:], q[:], ACT.Gelu_apprx_tanh))
                        act.wait(t)
                        made[f] = split(g_hi[f % 2][:], g_lo[f % 2][:], q[:], t, *freed.get(f - 2, ()))

                    def second_half(f):
                        pe.wait(made[f])
                        for r in range(RT):
                            terms = three(g_hi[f % 2][:, r * P:(r + 1) * P], g_lo[f % 2][:, r * P:(r + 1) * P],
                                          w2_hi[:, f, :], w2_lo[:, f, :])
                            for m_, (lhs, rhs) in enumerate(terms):
                                m = M.matmul(bank(4 + r), lhs, rhs, start=(f == 0 and m_ == 0),
                                             stop=(f == FT - 1 and m_ == 2))
                            if f == FT - 1 or r == RT - 1:
                                freed[f] = freed.get(f, ()) + (pe.mark(m),)

                    first_half(0)
                    for f in range(FT):
                        if f + 1 < FT:
                            first_half(f + 1)
                            side.tick()
                        elif more:
                            finish(operand(side.finish(), last["x"]))
                        second_half(f)
                        side.tick()
                    for r in range(RT):
                        dve.wait(freed[FT - 1][r])
                        t = dve.mark(V.tensor_tensor(residual[:, r, :], bank(4 + r), residual[:, r, :], ALU.add))
                    store_rows(0, x_mid[1], b, residual, t)
                    core.fence()
                    hidden.reset()

                got_bp = core.dma(PROJECTION + 2, bp[:], a["bp0"].partition_broadcast(P))
                wt = None

                def opened():
                    nonlocal wt
                    wt, w_step, kept = yield from quantised_weight(scope, "wp0", a["wp0"], o_rows, PROJECTION + 3,
                                                                   ring=hidden)
                    stepped = row_of(w_row[:], w_step, kept, (dve.sem, dve.n), ring=hidden)
                    pe.wait(kept)
                    dve.wait(stepped, got_bp)
                    return (yield from projected(0))

                first = Side(opened())
                stage = Ring([residual[:, r, :] for r in range(RT)] + [code[0][:], code[1][:]])
                weights = []
                for name, dram, width in (("w1", a["w1_t"], FF), ("w2", a["w2_t"], D)):
                    weight = Side(load_split_weight(scope, name, dram, stage, width))
                    while weight.chain is not None:
                        weight.tick()
                        first.tick(STEPS_LOAD_0)
                    weights.append(weight.value)
                (w1_hi, w1_lo, _), (w2_hi, w2_lo, _) = weights
                finish(operand(first.finish()))
                core.fence()
                hidden.reset()
                open_kept(0)
                with nc.Fori(0, B - 1) as b:
                    batch(b, True)
                batch(B - 1, False)
                core.release(0, B)
                core.fence()

        def out_projection_and_ffn_1():
            with ExitStack() as scope:
                o_cols = sbuf(scope, "o1_cols", [P, KT, S])
                o_hi = sbuf(scope, "o1_hi", [P, KT, S], F32R)
                o_lo = sbuf(scope, "o1_lo", [P, KT, S], F32R)
                rows = sbuf(scope, "f1_rows", [P, RT, D])
                delta = sbuf(scope, "o1_delta", [P, RT, D])
                bo = sbuf(scope, "o1_bo", [P, D])
                gamma = sbuf(scope, "o1_gamma", [P, D])
                beta = sbuf(scope, "o1_beta", [P, D])
                rs = sbuf(scope, "o1_rs", [P, 1])
                residual = sbuf(scope, "f1_residual", [P, RT, D])
                small = norm_small(scope, "f1")
                x_hi = sbuf(scope, "f1_x_hi", [P, KT, S], F32R)
                x_lo = sbuf(scope, "f1_x_lo", [P, KT, S], F32R)
                h_hi = sbuf(scope, "f1_h_hi", [P, KT, S], F32R)
                h_lo = sbuf(scope, "f1_h_lo", [P, KT, S], F32R)
                logits = sbuf(scope, "f1_logits", [P, RT, NE])
                top = sbuf(scope, "f1_top", [P, RT, NE])
                e2 = sbuf(scope, "f1_e2", [P, RT, 2])
                total = sbuf(scope, "f1_total", [P, RT])
                inverse = sbuf(scope, "f1_inverse", [P, RT])
                weight = sbuf(scope, "f1_weight", [P, RT])
                PROJECTION = 8

                def projected(b, *tokens):
                    got = [core.dma(PROJECTION + g, o_cols[:, g, :], at(o_t[1], b * NG + g + 1), *tokens)
                           for g in range(NG)]
                    got_x = load_rows(PROJECTION + NG, rows, x_mid[1], b, *tokens)
                    yield
                    for g in range(NG):
                        ready = split(o_hi[:, g, :], o_lo[:, g, :], o_cols[:, g, :], got[g])
                        if g % 2:
                            yield
                    yield from pause(PAUSE_O1)
                    for r in range(RT):
                        i, ps = banks.next()
                        terms = []
                        for k in range(KT):
                            terms += three(o_hi[:, k, r * P:(r + 1) * P], o_lo[:, k, r * P:(r + 1) * P],
                                           w_hi[:, k, :], w_lo[:, k, :])
                        done = products(ps, terms, ready, *banks.free[i])
                        dve.wait(done)
                        t = dve.mark(V.tensor_tensor(delta[:, r, :], ps, bo[:], ALU.add))
                        banks.free[i] = (t,)
                        dve.wait(t)
                        t = dve.mark(V.tensor_scalar(delta[:, r, :], delta[:, r, :], rs[:, 0:1], None, ALU.mult))
                        pool.wait(got_x)
                        u = pool.mark(G.tensor_tensor(rows[:, r, :], rows[:, r, :], beta[:], ALU.add))
                        yield
                    s = yield from layer_norm(delta, delta, small, t)
                    dve.wait(s, u)
                    for r in range(RT):
                        t = dve.mark(V.tensor_tensor(delta[:, r, :], delta[:, r, :], gamma[:], ALU.mult))
                        dve.wait(t)
                        t = dve.mark(V.tensor_tensor(rows[:, r, :], rows[:, r, :], delta[:, r, :], ALU.add))
                        yield
                    return (yield from layer_norm(rows, delta, small, t))

                def operand(s, *tokens):
                    return transposed(delta, lambda k, src, t: split(x_hi[:, k, :], x_lo[:, k, :], src, t, *tokens), s)

                def batch(b, more):
                    side = Side(iter(()))
                    act.wait(core.keep(0, b, 1))
                    for r in range(RT):
                        copied = act.mark(A.activation(residual[:, r, :], rows[:, r, :], ACT.Copy))
                    if more:
                        side = Side(projected(b + 1, copied))
                    for r in range(RT):
                        i, ps = banks.next()
                        terms = []
                        for k in range(KT):
                            terms += three(x_hi[:, k, r * P:(r + 1) * P], x_lo[:, k, r * P:(r + 1) * P],
                                           wg_hi[:, k, :], wg_lo[:, k, :])
                        done = products(ps[:, 0:NE], terms, *banks.free[i])
                        dve.wait(done)
                        t = dve.mark(V.tensor_copy(logits[:, r, :], ps[:, 0:NE]))
                        banks.free[i] = (t,)
                        dve.wait(t)
                        t = dve.mark(V.max(top[:, r, :], logits[:, r, :]))
                    side.tick()
                    dve.wait(t)
                    for r in range(RT):
                        t = dve.mark(V.tensor_scalar(e2[:, r, :], top[:, r, 0:2], top[:, r, 0:1], None, ALU.subtract))
                    act.wait(t)
                    t = act.mark(A.activation(e2[:], e2[:], ACT.Exp))
                    dve.wait(t)
                    t = dve.mark(V.tensor_reduce(total[:], e2[:], AX.X, ALU.add))
                    dve.wait(t)
                    t = dve.mark(V.reciprocal(inverse[:], total[:]))
                    dve.wait(t)
                    for r in range(RT):
                        t = dve.mark(V.tensor_scalar(e2[:, r, :], e2[:, r, :], inverse[:, r:r + 1], None, ALU.mult))
                    dve.wait(t)
                    weighted = dve.mark(V.tensor_reduce(weight[:], e2[:], AX.X, ALU.add))
                    side.tick()
                    for f in range(KT):
                        i, ps = banks.next()
                        terms = []
                        for k in range(KT):
                            terms += three(wu_hi[:, k, f * P:(f + 1) * P], wu_lo[:, k, f * P:(f + 1) * P],
                                           x_hi[:, k, :], x_lo[:, k, :])
                        done = products(ps, terms, *banks.free[i])
                        act.wait(done)
                        h = act.mark(A.activation(h_hi[:, f, :], ps, ACT.Relu))
                        dve.wait(h)
                        hidden = dve.mark(V.scalar_tensor_tensor(out=h_lo[:, f, :], in0=ps, scalar=0.0,
                                                                 in1=f32(h_hi[:, f, :]), op0=ALU.max,
                                                                 op1=ALU.subtract))
                        banks.free[i] = (hidden,)
                        side.tick(STEPS_FFN_1)
                    dve.wait(copied)
                    for r in range(RT):
                        i, ps = banks.next()
                        terms = []
                        for k in range(KT):
                            terms += three(x_hi[:, k, r * P:(r + 1) * P], x_lo[:, k, r * P:(r + 1) * P],
                                           we_hi[:, k, :], we_lo[:, k, :])
                        last = products(ps, terms, *banks.free[i])
                        dve.wait(last, weighted)
                        t = dve.mark(V.scalar_tensor_tensor(out=residual[:, r, :], in0=ps, scalar=weight[:, r:r + 1],
                                                            in1=residual[:, r, :], op0=ALU.mult, op1=ALU.add))
                        banks.free[i] = (t,)
                        side.tick(STEPS_FFN_1)
                    for r in range(RT):
                        i, ps = banks.next()
                        terms = []
                        for k in range(KT):
                            terms += three(h_hi[:, k, r * P:(r + 1) * P], h_lo[:, k, r * P:(r + 1) * P],
                                           wd_hi[:, k, :], wd_lo[:, k, :])
                        done = products(ps, terms, hidden, *banks.free[i])
                        dve.wait(done, t)
                        u = dve.mark(V.tensor_tensor(residual[:, r, :], ps, residual[:, r, :], ALU.add))
                        banks.free[i] = (u,)
                        side.tick(STEPS_LAST)
                        if r == RT - 2 and more:
                            finish(operand(side.finish(), last))
                    store_rows(0, out, b, residual, u)
                    end_loop()

                core.dma(20, bo[:], a["bo1"].partition_broadcast(P))
                core.dma(20, gamma[:], a["gamma"].partition_broadcast(P))
                core.dma(20, beta[:], a["beta"].partition_broadcast(P))
                got = core.dma(20, rs[:], a["rs"].partition_broadcast(P))
                dve.wait(got)
                dve.mark(V.tensor_scalar(rs[:], rs[:], 0.0, 0.3, ALU.max, ALU.min))
                stage = Ring([residual[:, r, :] for r in range(RT)] +
                             [sbuf(scope, f"f1_stage{i}", [P, D]) for i in range(4)])
                w_hi, w_lo, split_up = finish(load_split_weight(scope, "wo1", a["wo1_t"], stage, D))
                pe.wait(*split_up)
                first = Side(projected(0))
                weights = []
                for name, dram, width in (("wu", a["wu_t"], D), ("wd", a["wd_t"], D), ("we", a["we"], D),
                                          ("wg", a["wg_t"], NE)):
                    part = Side(load_split_weight(scope, name, dram, stage, width))
                    while part.chain is not None:
                        part.tick()
                        first.tick(STEPS_LOAD_1)
                    weights.append(part.value)
                (wu_hi, wu_lo, _), (wd_hi, wd_lo, _), (we_hi, we_lo, _), (wg_hi, wg_lo, _) = weights
                finish(operand(first.finish()))
                core.fence()
                banks.reset()
                open_kept(0)
                with nc.Fori(0, B - 1) as b:
                    batch(b, True)
                batch(B - 1, False)
                core.release(0, B)
                core.fence()

        kv_and_q_projection()
        attention(0)
        out_projection_and_ffn_0()
        with ExitStack() as scope:
            early = (sbuf(scope, "k_st10", [P, HPG, TP], F32R), sbuf(scope, "v_st10", [P, TT, P]))
            q_projection_1(early)
            attention(1, early)
        out_projection_and_ffn_1()


def laid_out(inputs):
    import numpy as np

    f = {k: np.asarray(v) for k, v in inputs.items()}
    c = np.ascontiguousarray
    columns = lambda v: c(v.reshape(KT, P).T)
    row = lambda v: c(v.reshape(-1))
    mask = np.pad(f["mask_BxS2_ik0"], ((0, 0), (0, TT * P - T)))
    return {
        "x": c(f["x"]), "ctx_t": c(f["ctx_2048"].transpose(0, 2, 1)),
        "mask_t": c(mask.reshape(B, TT, P).transpose(2, 0, 1)),
        "wq0": c(f["L0_xattn_wq"]), "bq0": columns(f["L0_xattn_bq"]),
        "wkv0_t": c(f["L0_xattn_wkv"].T),
        "bk0": columns(f["L0_xattn_bkv"][:D]), "bv0": row(f["L0_xattn_bkv"][D:]),
        "wp0": c(f["L0_xattn_wp"]), "bp0": row(f["L0_xattn_bp"]),
        "w1_t": c(f["L0_ffn_W1"].T), "w2_t": c(f["L0_ffn_W2"].T),
        "wq1_t": c(f["L1_xattn_Wq"].T), "bq1": columns(f["L1_xattn_bq"]),
        "wk1_t": c(f["L1_xattn_Wk"].T), "bk1": columns(f["L1_xattn_bk"]),
        "wv1_t": c(f["L1_xattn_Wv"].T), "bv1": row(f["L1_xattn_bv"]),
        "wo1_t": c(f["L1_xattn_Wo"].T), "bo1": row(f["L1_xattn_bo"]),
        "gamma": row(f["L1_xattn_ln_gamma"]), "beta": row(f["L1_xattn_ln_beta"]),
        "rs": c(f["L1_xattn_residual_scale"].reshape(1)),
        "wu_t": c(f["L1_ffn_W_up"].T), "wd_t": c(f["L1_ffn_W_down"].T),
        "wg_t": c(f["L1_ffn_W_gate"].T), "we": c(f["L1_ffn_W_expert"]),
    }


def kernel(**inputs):
    import concourse.bacc as bacc
    from concourse.bass_utils import run_bass_kernel_spmd

    nc = bacc.Bacc("TRN2", target_bir_lowering=False, num_devices=1)
    arrays = {f"in_{k}": v for k, v in laid_out(inputs).items()}
    args = {k[3:]: nc.dram_tensor(k, v.shape, mybir.dt.from_np(v.dtype), kind="ExternalInput").ap()
            for k, v in arrays.items()}
    result = nc.dram_tensor("result", (B, S, D), F32, kind="ExternalOutput").ap()
    build(nc, args, result)
    return run_bass_kernel_spmd(nc, [arrays], core_ids=[0]).results[0]["result"]
```
